# Optimizing a Trainium2 kernel written in Bass

```python
import numpy as np
import jax
import jax.numpy as jnp

def _softmax(x, axis=-1):
    return jax.nn.softmax(x, axis=axis)

def _gelu(x):
    return jax.nn.gelu(x, approximate=True)

def _silu(x):
    return jax.nn.silu(x)

def _sigmoid(x):
    return jax.nn.sigmoid(x)

def _layernorm(x, axis=-1, eps=1e-05):
    m = jnp.mean(x, axis=axis, keepdims=True)
    v = jnp.var(x, axis=axis, keepdims=True)
    return (x - m) / jnp.sqrt(v + eps)

def _scatter_add(tgt, idx, src, axis=0):
    return tgt.at[idx].add(src)

def _segment_sum(src, seg, n):
    return jax.ops.segment_sum(src, seg, n)
kernel_name = 'mk_adaln_attn_ffn_d1_seqx_r8_5ad9c4'

def setup_inputs(seed: int=0):
    np.random.seed(seed)
    _w = jnp.asarray

    def _rec_inputs():
        import jax
        import jax.numpy as jnp
        _rk = jax.random.key(seed)
        x = -0.000125 + 0.9999 * jax.random.normal(jax.random.fold_in(_rk, 1), (128, 32, 256), jnp.float32)
        _lenS = 32 - jax.random.randint(jax.random.fold_in(_rk, 7), (128,), 0, max(1, 32 // 4) + 1, jnp.int32)
        _lenS2 = 32 - jax.random.randint(jax.random.fold_in(_rk, 8), (128,), 0, max(1, 32 // 4) + 1, jnp.int32)
        cond_2048 = 7.82532e-05 + 0.0100527 * jax.random.normal(jax.random.fold_in(_rk, 11), (128, 256), jnp.float32)
        return (x, cond_2048)
    x, cond_2048 = _rec_inputs()

    def _L0_cond_setup():
        import jax, jax.numpy as jnp
        import numpy as np
        NUM_BLOCKS = 8
        NUM_LAYERS = 4
        EPS = 1e-06
        key = jax.random.key(seed)
        ks = jax.random.split(key, 6)
        B, S, H = (4, 512, 256)
        inputs = jax.random.normal(ks[0], (B, S, H), dtype=jnp.float32)
        query_vectors = jax.random.normal(ks[1], (NUM_LAYERS, H), dtype=jnp.float32) * 0.01
        lim = float(np.sqrt(6.0 / (H + H)))
        Wk = jax.random.uniform(ks[2], (H, H), minval=-lim, maxval=lim, dtype=jnp.float32)
        Wo = jax.random.uniform(ks[3], (H, H), minval=-lim, maxval=lim, dtype=jnp.float32)
        rms_weight = jnp.ones((H,), dtype=jnp.float32)
        ln_gamma = jnp.ones((H,), dtype=jnp.float32)
        ln_beta = jnp.zeros((H,), dtype=jnp.float32)
        return {'inputs': inputs, 'layer_idx': 1, 'rms_weight': rms_weight, 'query_vectors': query_vectors, 'Wk': Wk, 'Wo': Wo, 'ln_gamma': ln_gamma, 'ln_beta': ln_beta}
    _L0_cond_all = _L0_cond_setup()
    _L0_cond_in = {k: v for k, v in _L0_cond_all.items() if k in ('rms_weight', 'Wk', 'Wo', 'ln_gamma', 'ln_beta')}
    del _L0_cond_all

    def _L0_attn_setup():
        import jax, jax.numpy as jnp
        import numpy as np
        N_HEAD = 32
        HEAD_ID = 0
        MASKED_BIAS = -10000.0
        key = jax.random.key(seed)
        k1, k2, k3 = jax.random.split(key, 3)
        B, S, E = (1, 256, 256)
        hidden_states = jax.random.normal(k1, (B, S, E), dtype=jnp.float32)
        W_attn = jax.random.normal(k2, (E, 3 * E), dtype=jnp.float32) * (1.0 / np.sqrt(E))
        b_attn = jnp.zeros((3 * E,), dtype=jnp.float32)
        W_proj = jax.random.normal(k3, (E, E), dtype=jnp.float32) * (1.0 / np.sqrt(E))
        b_proj = jnp.zeros((E,), dtype=jnp.float32)
        return {'hidden_states': hidden_states, 'W_attn': W_attn, 'b_attn': b_attn, 'W_proj': W_proj, 'b_proj': b_proj}
    _L0_attn_all = _L0_attn_setup()
    _L0_attn_in = {k: v for k, v in _L0_attn_all.items() if k in ('W_attn', 'b_attn', 'W_proj', 'b_proj')}
    del _L0_attn_all

    def _L0_cond2_setup():
        import jax, jax.numpy as jnp
        import numpy as np
        B, T, D = (16, 128, 256)
        key = jax.random.key(seed)
        k0, k1, k2, k3 = jax.random.split(key, 4)
        scale = 1.0 / np.sqrt(D)
        return {'initial_state': jax.random.normal(k0, (B, D), jnp.float32), 'inputs': jax.random.normal(k1, (B, T, D), jnp.float32), 'W_ih': jax.random.normal(k2, (D, 3 * D), jnp.float32) * scale, 'W_hh': jax.random.normal(k3, (D, 3 * D), jnp.float32) * scale, 'b_ih': jnp.zeros((3 * D,), jnp.float32), 'b_hh': jnp.zeros((3 * D,), jnp.float32)}
    _L0_cond2_all = _L0_cond2_setup()
    _L0_cond2_in = {k: v for k, v in _L0_cond2_all.items() if k in ('W_ih', 'W_hh', 'b_ih', 'b_hh')}
    del _L0_cond2_all

    def _L0_ffn_setup():
        import jax, jax.numpy as jnp
        import numpy as np
        key = jax.random.key(seed)
        k1, k2, k3, k4 = jax.random.split(key, 4)
        B, S, D_IN, D_OUT = (4, 512, 256, 256)
        x = jax.random.normal(k1, (B, S, D_IN), dtype=jnp.float32)
        weight = jax.random.normal(k2, (D_OUT, D_IN), dtype=jnp.float32) * 0.02
        scale_weight = jax.random.uniform(k3, (D_OUT,), dtype=jnp.float32, minval=0.5, maxval=1.5)
        bias = jax.random.normal(k4, (D_OUT,), dtype=jnp.float32) * 0.02
        return {'x': x, 'weight': weight, 'scale_weight': scale_weight, 'bias': bias}
    _L0_ffn_all = _L0_ffn_setup()
    _L0_ffn_in = {k: v for k, v in _L0_ffn_all.items() if k in ('weight', 'scale_weight', 'bias')}
    del _L0_ffn_all
    return {'x': x, 'cond_2048': cond_2048, 'L0_cond_rms_weight': _L0_cond_in['rms_weight'], 'L0_cond_Wk': _L0_cond_in['Wk'], 'L0_cond_Wo': _L0_cond_in['Wo'], 'L0_cond_ln_gamma': _L0_cond_in['ln_gamma'], 'L0_cond_ln_beta': _L0_cond_in['ln_beta'], 'L0_attn_W_attn': _L0_attn_in['W_attn'], 'L0_attn_b_attn': _L0_attn_in['b_attn'], 'L0_attn_W_proj': _L0_attn_in['W_proj'], 'L0_attn_b_proj': _L0_attn_in['b_proj'], 'L0_cond2_W_ih': _L0_cond2_in['W_ih'], 'L0_cond2_W_hh': _L0_cond2_in['W_hh'], 'L0_cond2_b_ih': _L0_cond2_in['b_ih'], 'L0_cond2_b_hh': _L0_cond2_in['b_hh'], 'L0_ffn_weight': _L0_ffn_in['weight'], 'L0_ffn_scale_weight': _L0_ffn_in['scale_weight'], 'L0_ffn_bias': _L0_ffn_in['bias']}

def reference(x, cond_2048, L0_cond_rms_weight, L0_cond_Wk, L0_cond_Wo, L0_cond_ln_gamma, L0_cond_ln_beta, L0_attn_W_attn, L0_attn_b_attn, L0_attn_W_proj, L0_attn_b_proj, L0_cond2_W_ih, L0_cond2_W_hh, L0_cond2_b_ih, L0_cond2_b_hh, L0_ffn_weight, L0_ffn_scale_weight, L0_ffn_bias):
    import jax
    import jax.numpy as jnp

    def _L0_cond_ref(inputs, layer_idx, rms_weight, query_vectors, Wk, Wo, ln_gamma, ln_beta):
        import jax, jax.numpy as jnp
        import numpy as np
        NUM_BLOCKS = 8
        NUM_LAYERS = 4
        EPS = 1e-06
        B, S, H = inputs.shape
        block_size = max(1, S // NUM_BLOCKS)
        n_blocks = S // block_size
        block_repr = inputs.reshape(B, n_blocks, block_size, H).sum(axis=2)
        keys = jnp.einsum('bnh,kh->bnk', block_repr, Wk)
        rms = jnp.sqrt(jnp.mean(keys * keys, axis=-1, keepdims=True) + EPS)
        keys = keys / rms * rms_weight
        q = query_vectors[layer_idx]
        scores = jnp.einsum('bnh,h->bn', keys, q)
        attn = jax.nn.softmax(scores, axis=-1)
        attended = jnp.einsum('bn,bnh->bh', attn, block_repr)
        attended = jnp.broadcast_to(attended[:, None, :], (B, S, H))
        proj = jnp.einsum('bsh,kh->bsk', attended, Wo)
        x = inputs + proj
        mu = jnp.mean(x, axis=-1, keepdims=True)
        var = jnp.mean((x - mu) ** 2, axis=-1, keepdims=True)
        out = (x - mu) / jnp.sqrt(var + EPS) * ln_gamma + ln_beta
        return out

    def _L0_attn_ref(hidden_states, W_attn, b_attn, W_proj, b_proj):
        import jax, jax.numpy as jnp
        import numpy as np
        N_HEAD = 32
        HEAD_ID = 0
        MASKED_BIAS = -10000.0
        B, S, E = hidden_states.shape
        H = N_HEAD
        D = E // H
        m = 2.0 ** (-(8.0 / H) * (HEAD_ID + 1))
        qkv = hidden_states @ W_attn + b_attn
        q, k, v = jnp.split(qkv, 3, axis=-1)
        q = q.reshape(B, S, H, D).transpose(0, 2, 1, 3)
        k = k.reshape(B, S, H, D).transpose(0, 2, 1, 3)
        v = v.reshape(B, S, H, D).transpose(0, 2, 1, 3)
        scores = jnp.einsum('bhqd,bhkd->bhqk', q, k) / jnp.sqrt(jnp.float32(D))
        rows = jnp.arange(S)[:, None]
        cols = jnp.arange(S)[None, :]
        causal = cols <= rows
        scores = jnp.where(causal, scores, jnp.float32(MASKED_BIAS))
        alibi = jnp.where(causal, (cols - rows).astype(scores.dtype), 0.0)
        scores = scores + alibi * m
        probs = jax.nn.softmax(scores, axis=-1)
        attn = jnp.einsum('bhqk,bhkd->bhqd', probs, v)
        attn = attn.transpose(0, 2, 1, 3).reshape(B, S, E)
        out = attn @ W_proj + b_proj
        return out

    def _L0_cond2_ref(initial_state, inputs, W_ih, W_hh, b_ih, b_hh):
        import jax, jax.numpy as jnp
        import numpy as np
        B, T, D = (16, 128, 256)
        "ScanOverTime(GRU cell): sequential per-timestep module call with\n            dict-state passing; merge_dict_trees stacks the per-step\n            'state_predicted' tensors along axis=1 -> [B, T, D]."

        def cell(h, x):
            gi = x @ W_ih + b_ih
            gh = h @ W_hh + b_hh
            i_r, i_z, i_n = jnp.split(gi, 3, axis=-1)
            h_r, h_z, h_n = jnp.split(gh, 3, axis=-1)
            r = jax.nn.sigmoid(i_r + h_r)
            z = jax.nn.sigmoid(i_z + h_z)
            n = jnp.tanh(i_n + r * h_n)
            h_new = (1.0 - z) * n + z * h
            return (h_new, h_new)
        xs = jnp.swapaxes(inputs, 0, 1)
        _, hs = jax.lax.scan(cell, initial_state, xs)
        return jnp.swapaxes(hs, 0, 1)

    def _L0_ffn_ref(x, weight, scale_weight, bias):
        import jax, jax.numpy as jnp
        import numpy as np
        w = weight * scale_weight[:, None]
        out = jnp.einsum('bsi,oi->bso', x, w) + bias
        return out
    x = x + _L0_attn_ref(_L0_cond_ref(x, 1, L0_cond_rms_weight, cond_2048, L0_cond_Wk, L0_cond_Wo, L0_cond_ln_gamma, L0_cond_ln_beta), L0_attn_W_attn, L0_attn_b_attn, L0_attn_W_proj, L0_attn_b_proj)
    x = x + _L0_ffn_ref(_L0_cond2_ref(cond_2048, x, L0_cond2_W_ih, L0_cond2_W_hh, L0_cond2_b_ih, L0_cond2_b_hh), L0_ffn_weight, L0_ffn_scale_weight, L0_ffn_bias)
    return x

_drawn_inputs = setup_inputs


def setup_inputs(seed=0):
    import zlib

    import numpy as np

    out = dict(_drawn_inputs(seed))
    spreads = {'L0_cond_rms_weight': (1.0, 0.6),
     'L0_cond_ln_gamma': (1.0, 0.2),
     'L0_cond_ln_beta': (0.0, 0.1),
     'L0_attn_b_attn': (0.0, 0.1),
     'L0_attn_b_proj': (0.0, 0.1),
     'L0_cond2_b_ih': (0.0, 0.623),
     'L0_cond2_b_hh': (0.0, 0.8)}
    factors = {'L0_ffn_bias': 4.097}
    for name, (base, spread) in spreads.items():
        noise = np.random.default_rng([zlib.crc32(name.encode()), seed]).standard_normal(out[name].shape)
        drawn = base * np.exp(spread * noise) if base else spread * noise
        out[name] = jnp.asarray(drawn.astype(out[name].dtype))
    for name, factor in factors.items():
        out[name] = (out[name] * factor).astype(out[name].dtype)
    return out
```

```python
from contextlib import ExitStack

import numpy as np

import concourse.bass as bass
from concourse import mybir

ALU = mybir.AluOpType
ACT = mybir.ActivationFunctionType
AX_X = mybir.AxisListType.X
F32 = mybir.dt.float32
BF16 = mybir.dt.bfloat16

B, S, E = 128, 32, 256
NH, HD = 32, 8
NBLK = 8
P = 128
C = E // P
TB = P // S
GT = 4
GB = GT * TB
NG = B // GB
HG = 4
NQ = NH // HG
HW = NQ // 2
GC = GT * P
QT = NQ * S
VT = TB * NQ * HD
SLOT = GT * QT
MASKED = -10000.0
EPS = 1e-6
BIG = float(2.0 ** 100)
SCALE = float(np.float32(1.0) / np.sqrt(np.float32(HD)))
DMA = 16

V_GAMMA, V_BETA, V_BPROJ, V_FFNB, V_BIH, V_BHH = 0, 2, 4, 6, 8, 14
NVEC = 20
R_Q, R_RMS, R_BV, R_FSC = range(4)


def split_bf16(a):
    parts = []
    for _ in range(3):
        p = (a.view(np.uint32) & np.uint32(0xFFFF0000)).view(np.float32)
        parts.append(p)
        a = (a - p).astype(np.float32)
    return parts


def shape_constants():
    q, k = np.arange(S)[:, None], np.arange(S)[None, :]
    causal = k <= q
    slope = np.float32(2.0 ** (-(8.0 / NH)))
    alibi = np.where(causal, (k - q).astype(np.float32) * slope, np.float32(0)).astype(np.float32)
    parts = split_bf16(alibi)
    parts[0] = np.where(causal, parts[0], np.float32(BIG))
    bias = np.zeros((P, S), np.float32)
    bias[: 3 * S] = np.concatenate(parts, 0)
    pick = np.zeros((P, P), np.float32)
    for part in range(3):
        for r in range(S):
            pick[part * S + r, r::S] = 1.0
    floor = np.tile(np.where(causal, np.float32(3e38), np.float32(MASKED)), (TB, 1))
    spread = np.zeros((P, GC), np.float32)
    for b in range(GB):
        spread[b * NBLK:(b + 1) * NBLK, b * S:(b + 1) * S] = 1.0
    ident = np.eye(P, dtype=np.float32)
    return np.ascontiguousarray(np.concatenate([ident, pick, bias, floor, spread], 1).astype(np.float32))


K_ID, K_PICK, K_BIAS, K_FLOOR, K_SPREAD = 0, P, 2 * P, 2 * P + S, 2 * P + 2 * S
NCONST = 2 * P + 2 * S + GC


def adaln_attn_gru_ffn(nc, x_tok, x_feat, cond_t, wkwo, wq, wk, wv, wp, wih, whh, wf, vecs, rows, bqk, consts, out):
    ctx = ExitStack()
    with ctx:
        def sb(name, shape, dt=F32):
            return ctx.enter_context(nc.sbuf_tensor(name, shape, dt))

        def sem(name):
            return ctx.enter_context(nc.semaphore(name))

        xf = sb("xf", [P, C, S, B])
        xg = sb("xg", [P, GT, E])
        y = sb("y", [P, GT, E])
        yT = sb("yT", [P, C, GC])
        qn = sb("qn", [P, GT, QT])
        kn = sb("kn", [P, GT, QT])
        vn = sb("vn", [P, GT, E])
        qbd = sb("qbd", [P, GT, NQ, TB, S])
        kbd = sb("kbd", [P, HG, GT, QT])
        vbd = sb("vbd", [P, HG + 1, GT, VT])
        sc = sb("sc", [P, 2, NH * S])
        pT = sb("pT", [P, NQ, P])
        mx = sb("mx", [P, 2, NH])
        rden = sb("rden", [P, NH])
        on = sb("on", [P, E])
        oT = sb("oT", [P, C, P])
        bw = sb("bw", [P, NG, E])
        kw_sb = sb("kw_sb", [P, 2, E])
        junk = sb("junk", [P, 2, E])
        blkT = sb("blkT", [P, C, B, NBLK])
        ssq = sb("ssq", [P, NG])
        dotq = sb("dotq", [P, NG])
        rinv = sb("rinv", [P, NG])
        cs = sb("cs", [P, NG])
        cT = sb("cT", [NG, P])
        cmx = sb("cmx", [NG, GB])
        csum = sb("csum", [NG, GB])
        aS = sb("aS", [P, NG + 1])
        ra = sb("ra", [P, GC])
        st = sb("st", [P, GT, 6])
        mv = sb("mv", [P, GT, 2])
        rstd = sb("rstd", [P, GT])
        minus_half = sb("minus_half", [P, NG])
        eps_t = sb("eps_t", [P, GT])
        wqr = sb("wqr", [P, E])
        w_kwo = sb("w_kwo", [P, C, 2 * E])
        w_q, w_k, w_v, w_p, w_f = (sb(n, [P, C, E]) for n in ("w_q", "w_k", "w_v", "w_p", "w_f"))
        w_ih = sb("w_ih", [P, C, 3 * E])
        w_hh = sb("w_hh", [P, C, 3 * E])
        vec = sb("vec", [P, NVEC])
        brz = sb("brz", [P, 4])
        row = sb("row", [P, 4, E])
        bq_t = sb("bq_t", [P, 2, QT])
        kst = sb("kst", [P, NCONST])
        pick = sb("pick", [P, P], BF16)
        bias_t = sb("bias_t", [P, HW * HG, S], BF16)
        hT = sb("hT", [P, 2, C, B])
        rg = sb("rg", [P, C, B])
        zg = sb("zg", [P, C, B])
        zc = sb("zc", [P, C, B])
        zh = sb("zh", [P, C, B])
        npre = sb("npre", [P, C, B])
        ng = sb("ng", [P, C, B])
        ost = sb("ost", [P, 2, C, B])

        ident = kst[:, K_ID:K_ID + P]
        floor_t = kst[:, K_FLOOR:K_FLOOR + S]
        spread = kst[:, K_SPREAD:K_SPREAD + GC]

        ps_s = ctx.enter_context(nc.psum_tensor("ps_s", [P, 1024], F32))
        ps_t = ctx.enter_context(nc.psum_tensor("ps_t", [P, 1024], F32))
        ps_o = ctx.enter_context(nc.psum_tensor("ps_o", [P, 512], F32))
        ps_m = ctx.enter_context(nc.psum_tensor("ps_m", [P, 512], F32))
        ps_a = ctx.enter_context(nc.psum_tensor("ps_a", [P, 1024], F32))

        l_xf = [[sem(f"l_xf{c}{k}") for k in range(4)] for c in range(C)]
        l_xg = sem("l_xg")
        l_kwo = sem("l_kwo")
        l_small = sem("l_small")
        l_attn = sem("l_attn")
        l_gru = sem("l_gru")
        zeroed = sem("zeroed")
        consts_cast = sem("consts_cast")
        blk_sum = sem("blk_sum")
        wq_done = sem("wq_done")
        kw_mm = sem("kw_mm")
        kw_out = sem("kw_out")
        kw_red = sem("kw_red")
        c_step = sem("c_step")
        c_mm = sem("c_mm")
        c_exp = sem("c_exp")
        a_ready = sem("a_ready")
        ra_ready = sem("ra_ready")
        r_mm = sem("r_mm")
        z_done = sem("z_done")
        bn_done = sem("bn_done")
        eps_added = sem("eps_added")
        y_done = sem("y_done")
        yt_mm = sem("yt_mm")
        yt_out = sem("yt_out")
        q_mm = sem("q_mm")
        k_mm = sem("k_mm")
        v_mm = sem("v_mm")
        q_out = sem("q_out")
        k_out = sem("k_out")
        v_out = sem("v_out")
        k_in = [sem("k_in0"), sem("k_in1")]
        q_in = [sem("q_in0"), sem("q_in1")]
        v_in = [sem("v_in0"), sem("v_in1")]
        sc_mm = sem("sc_mm")
        sc_out = sem("sc_out")
        sc_max = sem("sc_max")
        sc_sub = sem("sc_sub")
        sc_exp = sem("sc_exp")
        pt_mm = sem("pt_mm")
        pt_out = sem("pt_out")
        pv_mm = sem("pv_mm")
        den_inv = sem("den_inv")
        o_norm = sem("o_norm")
        ot_mm = sem("ot_mm")
        ot_out = sem("ot_out")
        x1_mm = sem("x1_mm")
        x1_out = sem("x1_out")
        w_ready = sem("w_ready")
        g_r = sem("g_r")
        g_z = sem("g_z")
        g_n = sem("g_n")
        s_r = sem("s_r")
        s_z = sem("s_z")
        zc_done = sem("zc_done")
        zh_done = sem("zh_done")
        rh_done = sem("rh_done")
        npre_done = sem("npre_done")
        n_done = sem("n_done")
        nz_done = sem("nz_done")
        h_done = sem("h_done")
        f_mm = sem("f_mm")
        f_out = sem("f_out")
        stored = [sem("stored0"), sem("stored1")]

        block = ctx.enter_context(nc.Block())

        def x_group(g):
            return x_tok[bass.ds(g * GT, GT), :, :].rearrange("t p e -> p t e")

        def gate_bank(which, p):
            return {"r": (ps_s[:, 0:512], ps_s[:, 512:1024]), "z": (ps_t[:, 0:512], ps_t[:, 512:1024]),
                    "n": (ps_a[:, 0:512], ps_a[:, 512:1024])}[which][p]

        @block.sync
        def _(sp):
            for c in range(C):
                for k in range(4):
                    t = slice(k * (S // 4), (k + 1) * (S // 4))
                    sp.dma_start(xf[:, c, t, :], x_feat[c, :, t, :]).then_inc(l_xf[c][k], DMA)
                if c == 0:
                    sp.dma_start(w_kwo[:, :, :], wkwo).then_inc(l_kwo, DMA)
                    sp.dma_start(row[:, :, :], rows).then_inc(l_small, DMA)
                    sp.dma_start(vec[:, :], vecs).then_inc(l_small, DMA)
                    sp.dma_start(kst[:, :], consts).then_inc(l_small, DMA)
            sp.dma_start(xg[:, :, :], x_group(0)).then_inc(l_xg, DMA)
            for dst, src in ((w_q, wq), (w_k, wk), (w_v, wv), (w_p, wp)):
                sp.dma_start(dst[:, :, :], src).then_inc(l_attn, DMA)
            sp.dma_start(bq_t[:, :, :], bqk).then_inc(l_attn, DMA)
            for dst, src in ((w_ih, wih), (w_hh, whh), (w_f, wf)):
                sp.dma_start(dst[:, :, :], src).then_inc(l_gru, DMA)
            sp.dma_start(hT[:, 1, :, :], cond_t).then_inc(l_gru, DMA)
            sp.wait_ge(zeroed, 3)

            def move_k(half):
                cols = slice(half * (SLOT // 2), (half + 1) * (SLOT // 2))
                for j in range(HG):
                    kflat = kn[:, :, :].rearrange("p t n -> p (t n)")
                    kd = kbd[:, j, :, :].rearrange("p t n -> p (t n)")
                    sp.dma_start(kd[j:P:HG, cols], kflat[j:P:HG, cols]).then_inc(k_in[half], DMA)

            def move_v(half):
                tiles = slice(2 * half, 2 * half + 2)
                for b in range(TB):
                    for h in range(HG):
                        w = NQ * HD
                        sp.dma_start(vbd[32 * h:32 * h + 32, h, tiles, b * w:(b + 1) * w],
                                     vn[32 * b:32 * b + 32, tiles, h * w:(h + 1) * w]).then_inc(v_in[half], DMA)

            sp.wait_ge(z_done, 2)
            sp.dma_start(xg[:, :, :], x_group(1)).then_inc(l_xg, DMA)
            sp.wait_ge(k_out, 2)
            move_k(0)
            move_k(1)
            sp.wait_ge(v_out, 2)
            move_v(0)
            move_v(1)

            def group_loads(g, more):
                if more:
                    sp.wait_ge(z_done, 2 * g + 4)
                    sp.dma_start(xg[:, :, :], x_group(g + 2)).then_inc(l_xg, DMA)
                sp.wait_ge(k_out, 2 * g + 4)
                sp.wait_ge(sc_mm, 8 * g + 4)
                move_k(0)
                sp.wait_ge(sc_mm, 8 * g + 8)
                move_k(1)
                sp.wait_ge(v_out, 2 * g + 3)
                sp.wait_ge(pv_mm, 4 * g + 2)
                move_v(0)
                sp.wait_ge(pv_mm, 4 * g + 4)
                sp.wait_ge(v_out, 2 * g + 4)
                move_v(1)

            with sp.Fori(0, NG - 2) as g:
                group_loads(g, True)
            group_loads(NG - 2, False)

            def store(t, p):
                sp.wait_ge(f_out, 2 * t + 2)
                sp.dma_start(out[bass.ds(t, 1), :, :, :].rearrange("o p c b -> (o p) c b"),
                             ost[:, p, :, :]).then_inc(stored[p], DMA)

            with sp.Fori(0, S // 2) as j:
                store(2 * j, 0)
                store(2 * j + 1, 1)
            sp.wait_ge(stored[0], DMA * (S // 2))
            sp.wait_ge(stored[1], DMA * (S // 2))

        @block.gpsimd
        def _(pool):
            nc.gpsimd.memset(qbd[:, :, :, :, :], 0.0).then_inc(zeroed, 1)
            nc.gpsimd.memset(kbd[:, :, :, :], 0.0).then_inc(zeroed, 1)
            nc.gpsimd.memset(minus_half[:, :], -0.5).then_inc(eps_added, 1)
            nc.gpsimd.memset(eps_t[:, :], EPS).then_inc(eps_added, 1)
            pool.wait_ge(eps_added, 2)

            def inverse_std(k):
                pool.wait_ge(bn_done, 3 * k + 2)
                nc.gpsimd.tensor_tensor(rstd[:, :], mv[:, :, 1], eps_t[:, 0:GT], ALU.add).then_inc(eps_added, 1)
                pool.wait_ge(eps_added, k + 3)
                nc.gpsimd.tensor_tensor(rstd[:, :], rstd[:, :], minus_half[:, 0:GT], ALU.pow).then_inc(bn_done, 1)

            pool.wait_ge(c_step, 1)
            nc.gpsimd.tensor_tensor(rinv[:, :], rinv[:, :], minus_half[:, :], ALU.pow).then_inc(c_step, 1)
            inverse_std(0)
            inverse_std(1)

            with pool.Fori(0, NG - 2) as g:
                inverse_std(g + 2)

        @block.scalar
        def _(act):
            def copy_out(dst, src):
                return nc.scalar.activation(dst, src, ACT.Copy)

            for g in range(NG):
                act.wait_ge(kw_mm, g + 1)
                if g >= 2:
                    act.wait_ge(kw_red, 2 * (g - 1))
                copy_out(kw_sb[:, g % 2, :], ps_a[:, (g % 2) * 512:(g % 2) * 512 + E]).then_inc(kw_out, 1)
                copy_out(bw[:, g, :], ps_a[:, (g % 2) * 512 + E:(g % 2) * 512 + 2 * E]).then_inc(kw_out, 1)
            act.wait_ge(c_step, 5)
            nc.scalar.activation(cT[:, :], cT[:, :], ACT.Exp).then_inc(c_exp, 1)

            def transpose_out(k):
                for c in range(C):
                    act.wait_ge(yt_mm, C * k + c + 1)
                    nc.scalar.activation(yT[:, c, :], ps_a[:, c * 512:(c + 1) * 512], ACT.Identity,
                                         bias=vec[:, V_BETA + c:V_BETA + c + 1],
                                         scale=vec[:, V_GAMMA + c:V_GAMMA + c + 1]).then_inc(yt_out, 1)

            def place_q(k, half):
                act.wait_ge(q_out, 2 * k + 2)
                for b in range(TB):
                    part, tiles = slice(32 * b, 32 * b + 32), slice(2 * half, 2 * half + 2)
                    copy_out(qbd[part, tiles, :, b, :].rearrange("p t q s -> p (t q) s"),
                             qn[part, tiles, :].rearrange("p t (q s) -> p (t q) s", s=S)).then_inc(q_in[half], 1)

            def softmax_exp(n, p):
                for h in range(2):
                    act.wait_ge(sc_sub, 2 * n + h + 1)
                    part = sc[:, p, h * 512:(h + 1) * 512]
                    nc.scalar.activation(part, part, ACT.Exp).then_inc(sc_exp, 1)

            def probs_out(n):
                for h in range(2):
                    act.wait_ge(pt_mm, 2 * n + h + 1)
                    act.wait_ge(pv_mm, n)
                    copy_out(pT[:, h * HW:(h + 1) * HW, :].rearrange("p q n -> p (q n)"),
                             ps_t[:, h * 512:(h + 1) * 512]).then_inc(pt_out, 1)

            def attn_out(n):
                act.wait_ge(ot_mm, n + 1)
                copy_out(oT[:, :, :].rearrange("p c n -> p (c n)"), ps_m[:, 0:E]).then_inc(ot_out, 1)

            act.wait_ge(l_small, 3 * DMA)
            transpose_out(0)
            act.wait_ge(zeroed, 3)
            place_q(0, 0)
            place_q(0, 1)
            softmax_exp(0, 0)
            probs_out(0)

            def tile_step(g, i, ahead):
                n = GT * g + i
                last = not ahead and i == GT - 1
                if ahead and i == 0:
                    transpose_out(g + 1)
                if not last:
                    softmax_exp(n + 1, (i + 1) % 2)
                attn_out(n)
                if not last:
                    probs_out(n + 1)
                if ahead and i == 1:
                    act.wait_ge(sc_mm, 8 * g + 4)
                    place_q(g + 1, 0)
                if ahead and i == 2:
                    act.wait_ge(sc_mm, 8 * g + 8)
                    place_q(g + 1, 1)

            with act.Fori(0, NG - 1) as g:
                for i in range(GT):
                    tile_step(g, i, True)
            for i in range(GT):
                tile_step(NG - 1, i, False)

            def gates(t, p):
                for gate, dst, mm, done, b0 in (("r", rg, g_r, s_r, 0), ("z", zg, g_z, s_z, 2)):
                    act.wait_ge(mm, t + 1)
                    for c in range(C):
                        nc.scalar.activation(dst[:, c, :], gate_bank(gate, p)[:, c * B:(c + 1) * B], ACT.Sigmoid,
                                             bias=brz[:, b0 + c:b0 + c + 1]).then_inc(done, 1)
                for c in range(C):
                    act.wait_ge(npre_done, C * t + c + 1)
                    nc.scalar.activation(ng[:, c, :], npre[:, c, :], ACT.Tanh).then_inc(n_done, 1)

            act.wait_ge(w_ready, 2)
            gates(0, 0)
            with act.Fori(0, (S - 2) // 2) as j:
                gates(2 * j + 1, 1)
                gates(2 * j + 2, 0)
            gates(S - 1, 1)

        @block.vector
        def _(dve):
            nc.vector.memset(vbd[:, 0:HG, :, :], 0.0)
            nc.vector.memset(aS[:, NG:NG + 1], 0.0)
            ones = vbd[:, HG, :, :].rearrange("p t (n d) -> p (t n) d", d=HD)
            nc.vector.memset(ones, 0.0).then_inc(consts_cast, 1)
            dve.wait_ge(consts_cast, 1)
            for h in range(HG):
                last = nc.vector.memset(ones[32 * h:32 * h + 32, :, h:h + 1], 1.0)
            last.then_inc(zeroed, 1)
            dve.wait_ge(l_small, 3 * DMA)
            nc.vector.tensor_copy(pick[:, :], kst[:, K_PICK:K_PICK + P]).then_inc(consts_cast, 1)
            nc.vector.tensor_copy(bias_t[:, :, :], kst[:, K_BIAS:K_BIAS + S].unsqueeze(1).to_broadcast(
                [P, HW * HG, S])).then_inc(consts_cast, 1)
            nc.vector.tensor_tensor(wqr[:, :], row[:, R_Q, :], row[:, R_RMS, :], ALU.mult).then_inc(wq_done, 1)

            for c in range(C):
                for k in range(4):
                    dve.wait_ge(l_xf[c][k], DMA)
                    n0, n1 = k * NBLK // 4, (k + 1) * NBLK // 4
                    w = S // NBLK
                    nc.vector.tensor_reduce(
                        blkT[:, c, :, n0:n1].rearrange("p b n -> p n b"),
                        xf[:, c, n0 * w:n1 * w, :].rearrange("p (n w) b -> p n b w", w=w),
                        axis=AX_X, op=ALU.add).then_inc(blk_sum, 1)

            dve.wait_ge(wq_done, 1)
            for g in range(NG):
                dve.wait_ge(kw_out, 2 * g + 1)
                if g:
                    dve.wait_ge(kw_red, 2 * g)
                kk = kw_sb[:, g % 2, :]
                nc.vector.tensor_tensor_reduce(out=junk[:, 0, :], in0=kk, in1=kk, scale=1.0, scalar=0.0,
                                               op0=ALU.mult, op1=ALU.add,
                                               accum_out=ssq[:, g:g + 1]).then_inc(kw_red, 1)
                nc.vector.tensor_tensor_reduce(out=junk[:, 1, :], in0=kk, in1=wqr[:, :], scale=1.0, scalar=0.0,
                                               op0=ALU.mult, op1=ALU.add,
                                               accum_out=dotq[:, g:g + 1]).then_inc(kw_red, 1)
            dve.wait_ge(kw_red, 2 * NG)
            nc.vector.tensor_scalar(rinv[:, :], ssq[:, :], 1.0 / E, EPS, ALU.mult, ALU.add).then_inc(c_step, 1)
            dve.wait_ge(c_step, 1)
            dve.wait_ge(c_step, 2)
            nc.vector.tensor_tensor(cs[:, :], dotq[:, :], rinv[:, :], ALU.mult).then_inc(c_step, 1)
            dve.wait_ge(c_mm, 1)
            cps = ps_m[0:NG, 0:P].rearrange("g (b n) -> g b n", n=NBLK)
            cTv = cT[:, :].rearrange("g (b n) -> g b n", n=NBLK)
            nc.vector.tensor_reduce(cmx[:, :], cps, axis=AX_X, op=ALU.max).then_inc(c_step, 1)
            dve.wait_ge(c_step, 4)
            nc.vector.tensor_tensor(cTv, cps, cmx[:, :].unsqueeze(2).to_broadcast([NG, GB, NBLK]),
                                    ALU.subtract).then_inc(c_step, 1)
            dve.wait_ge(c_exp, 1)
            nc.vector.tensor_reduce(csum[:, :], cTv, axis=AX_X, op=ALU.add).then_inc(c_step, 1)
            dve.wait_ge(c_step, 6)
            nc.vector.reciprocal(csum[:, :], csum[:, :]).then_inc(c_step, 1)
            dve.wait_ge(c_step, 7)
            nc.vector.tensor_tensor(cTv, cTv, csum[:, :].unsqueeze(2).to_broadcast([NG, GB, NBLK]),
                                    ALU.mult).then_inc(c_step, 1)
            dve.wait_ge(c_mm, 2)
            nc.vector.tensor_copy(aS[:, 0:NG], ps_m[:, P:P + NG]).then_inc(a_ready, 1)

            dve.wait_ge(a_ready, 1)
            def select_blocks(k):
                dve.wait_ge(r_mm, 2 * k)
                nc.vector.tensor_scalar(ra[:, :], spread, aS[:, bass.ds(k, 1)], None, ALU.mult).then_inc(ra_ready, 1)

            def layer_norm(k):
                dve.wait_ge(l_xg, DMA * (k + 1))
                for h in range(2):
                    dve.wait_ge(r_mm, 2 * k + h + 1)
                    if h == 0:
                        dve.wait_ge(yt_mm, C * k)
                    nc.vector.tensor_tensor(y[:, 2 * h:2 * h + 2, :].rearrange("p t e -> p (t e)"),
                                            xg[:, 2 * h:2 * h + 2, :].rearrange("p t e -> p (t e)"),
                                            ps_a[:, h * 512:(h + 1) * 512], ALU.add).then_inc(z_done, 1)
                for i in range(GT):
                    dve.wait_ge(z_done, 2 * k + i // 2 + 1)
                    last = nc.vector.bn_stats(st[:, i, :], y[:, i, :])
                last.then_inc(bn_done, 1)
                dve.wait_ge(bn_done, 3 * k + 1)
                select_blocks(k + 1)
                for i in range(GT):
                    last = nc.vector.bn_aggr(mv[:, i, :], st[:, i, :])
                last.then_inc(bn_done, 1)
                dve.wait_ge(bn_done, 3 * k + 2)
                dve.wait_ge(bn_done, 3 * k + 3)
                for i in range(GT):
                    nc.vector.tensor_scalar(y[:, i, :], y[:, i, :], mv[:, i, 0:1], rstd[:, i:i + 1],
                                            ALU.subtract, ALU.mult).then_inc(y_done, 1)

            def bank_as_tiles(h):
                return ps_a[:, h * 512:(h + 1) * 512].rearrange("p (t n) -> p t n", t=GT)

            def q_bias(k):
                w = HW * S
                for h in range(2):
                    dve.wait_ge(q_mm, 2 * k + h + 1)
                    if h == 0:
                        dve.wait_ge(q_in[1], TB * k)
                    nc.vector.scalar_tensor_tensor(
                        qn[:, :, h * w:(h + 1) * w], bank_as_tiles(h), SCALE,
                        bq_t[:, 0, h * w:(h + 1) * w].unsqueeze(1).to_broadcast([P, GT, w]),
                        ALU.mult, ALU.add).then_inc(q_out, 1)

            def k_bias(k):
                w = HW * S
                for h in range(2):
                    dve.wait_ge(k_mm, 2 * k + h + 1)
                    if h == 0:
                        dve.wait_ge(k_in[0], HG * DMA * k)
                        dve.wait_ge(k_in[1], HG * DMA * k)
                    nc.vector.tensor_tensor(
                        kn[:, :, h * w:(h + 1) * w], bank_as_tiles(h),
                        bq_t[:, 1, h * w:(h + 1) * w].unsqueeze(1).to_broadcast([P, GT, w]),
                        ALU.add).then_inc(k_out, 1)

            def v_bias(k):
                for h in range(2):
                    dve.wait_ge(v_mm, 2 * k + h + 1)
                    if h == 0:
                        dve.wait_ge(v_in[0], 16 * DMA * k)
                        dve.wait_ge(v_in[1], 16 * DMA * k)
                    nc.vector.tensor_tensor(
                        vn[:, 2 * h:2 * h + 2, :], ps_a[:, h * 512:(h + 1) * 512].rearrange("p (t e) -> p t e", t=2),
                        row[:, R_BV, :].unsqueeze(1).to_broadcast([P, 2, E]), ALU.add).then_inc(v_out, 1)

            def softmax_shift(n, p):
                halves = [(h, sc[:, p, h * 512:(h + 1) * 512].rearrange("p (h k) -> p h k", k=S),
                           mx[:, p, h * NH // 2:(h + 1) * NH // 2]) for h in range(2)]
                for h, part, _ in halves:
                    dve.wait_ge(sc_mm, 2 * n + h + 1)
                    nc.vector.tensor_tensor(part, ps_s[:, h * 512:(h + 1) * 512].rearrange("p (h k) -> p h k", k=S),
                                            floor_t.unsqueeze(1).to_broadcast([P, NH // 2, S]),
                                            ALU.min).then_inc(sc_out, 1)
                for h, part, m in halves:
                    dve.wait_ge(sc_out, 2 * n + h + 1)
                    nc.vector.tensor_reduce(m, part, axis=AX_X, op=ALU.max).then_inc(sc_max, 1)
                for h, part, m in halves:
                    dve.wait_ge(sc_max, 2 * n + h + 1)
                    nc.vector.tensor_tensor(part, part, m.unsqueeze(2).to_broadcast([P, NH // 2, S]),
                                            ALU.subtract).then_inc(sc_sub, 1)

            def normalise(n):
                dve.wait_ge(pv_mm, n + 1)
                o5 = ps_o[:, 0:NQ * 40].rearrange("p (q s d) -> p q s d", q=NQ, s=HG + 1)
                nc.vector.reciprocal(rden[:, :].rearrange("p (q s) -> p q s", s=HG), o5[:, :, HG, 0:HG]).then_inc(den_inv, 1)
                dve.wait_ge(den_inv, n + 1)
                nc.vector.tensor_tensor(
                    on[:, :].rearrange("p (q s d) -> p q s d", q=NQ, s=HG), o5[:, :, 0:HG, :],
                    rden[:, :].rearrange("p (q s) -> p q s", s=HG).unsqueeze(3).to_broadcast([P, NQ, HG, HD]),
                    ALU.mult).then_inc(o_norm, 1)

            def residual(n):
                dve.wait_ge(x1_mm, n + 1)
                for c in range(C):
                    xs = xf[:, c, :, bass.ds(n * TB, TB)].rearrange("p t b -> p b t")
                    nc.vector.scalar_tensor_tensor(
                        xs, ps_m[:, E + c * P:E + (c + 1) * P].rearrange("p (b t) -> p b t", b=TB),
                        vec[:, V_BPROJ + c:V_BPROJ + c + 1], xs, ALU.add, ALU.add).then_inc(x1_out, 1)

            select_blocks(0)
            layer_norm(0)
            dve.wait_ge(l_gru, 4 * DMA)
            nc.vector.tensor_tensor(w_f[:, :, :], w_f[:, :, :],
                                    row[:, R_FSC, :].unsqueeze(1).to_broadcast([P, C, E]), ALU.mult).then_inc(w_ready, 1)
            nc.vector.tensor_tensor(brz[:, :], vec[:, V_BIH:V_BIH + 4], vec[:, V_BHH:V_BHH + 4],
                                    ALU.add).then_inc(w_ready, 1)
            dve.wait_ge(l_attn, 5 * DMA)
            nc.vector.tensor_scalar(bq_t[:, 0, :], bq_t[:, 0, :], SCALE, None, ALU.mult).then_inc(w_ready, 1)

            dve.wait_ge(w_ready, 3)
            q_bias(0)
            k_bias(0)
            v_bias(0)
            layer_norm(1)
            softmax_shift(0, 0)

            def tile_step(g, i, ahead, norm_ahead):
                n = GT * g + i
                if ahead or i < GT - 1:
                    softmax_shift(n + 1, (i + 1) % 2)
                normalise(n)
                if ahead and i == 0:
                    q_bias(g + 1)
                if ahead and i == 1:
                    k_bias(g + 1)
                if ahead and i == 2:
                    v_bias(g + 1)
                if norm_ahead and i == 3:
                    layer_norm(g + 2)
                residual(n)

            with dve.Fori(0, NG - 2) as g:
                for i in range(GT):
                    tile_step(g, i, True, True)
            for g in (NG - 2, NG - 1):
                for i in range(GT):
                    tile_step(g, i, g == NG - 2, False)

            def state(t, p):
                old, new = hT[:, 1 - p, :, :], hT[:, p, :, :]
                dve.wait_ge(s_z, C * t + C)
                nc.vector.tensor_scalar(zc[:, :, :], zg[:, :, :], -1.0, 1.0, ALU.mult, ALU.add).then_inc(zc_done, 1)
                nc.vector.tensor_tensor(zh[:, :, :], zg[:, :, :], old, ALU.mult).then_inc(zh_done, 1)
                dve.wait_ge(g_n, t + 1)
                for c in range(C):
                    dve.wait_ge(s_r, C * t + c + 1)
                    nc.vector.scalar_tensor_tensor(rg[:, c, :], ps_o[:, c * B:(c + 1) * B],
                                                   vec[:, V_BHH + 4 + c:V_BHH + 5 + c], rg[:, c, :],
                                                   ALU.add, ALU.mult).then_inc(rh_done, 1)
                for c in range(C):
                    dve.wait_ge(rh_done, C * t + c + 1)
                    nc.vector.scalar_tensor_tensor(npre[:, c, :], gate_bank("n", p)[:, c * B:(c + 1) * B],
                                                   vec[:, V_BIH + 4 + c:V_BIH + 5 + c], rg[:, c, :],
                                                   ALU.add, ALU.add).then_inc(npre_done, 1)
                dve.wait_ge(zc_done, t + 1)
                for c in range(C):
                    dve.wait_ge(n_done, C * t + c + 1)
                    nc.vector.tensor_tensor(ng[:, c, :], ng[:, c, :], zc[:, c, :], ALU.mult).then_inc(nz_done, 1)
                dve.wait_ge(zh_done, t + 1)
                for c in range(C):
                    dve.wait_ge(nz_done, C * t + c + 1)
                    nc.vector.tensor_tensor(new[:, c, :], ng[:, c, :], zh[:, c, :], ALU.add).then_inc(h_done, 1)

            def emit(t, p):
                dve.wait_ge(f_mm, t + 1)
                for c in range(C):
                    nc.vector.scalar_tensor_tensor(
                        ost[:, p, c, :], ps_m[:, c * B:(c + 1) * B], vec[:, V_FFNB + c:V_FFNB + c + 1],
                        xf[:, c, bass.ds(t, 1), :].rearrange("p o b -> p (o b)"),
                        ALU.add, ALU.add).then_inc(f_out, 1)

            dve.wait_ge(x1_out, C * (B // TB))
            state(0, 0)
            state(1, 1)
            emit(0, 0)
            state(2, 0)
            emit(1, 1)
            with dve.Fori(1, (S - 2) // 2) as j:
                state(2 * j + 1, 1)
                dve.wait_ge(stored[0], DMA * j)
                emit(2 * j, 0)
                state(2 * j + 2, 0)
                dve.wait_ge(stored[1], DMA * j)
                emit(2 * j + 1, 1)
            state(S - 1, 1)
            dve.wait_ge(stored[0], DMA * (S // 2 - 1))
            emit(S - 2, 0)
            dve.wait_ge(stored[1], DMA * (S // 2 - 1))
            emit(S - 1, 1)

        @block.tensor
        def _(pe):
            pe.wait_ge(l_kwo, DMA)
            pe.wait_ge(blk_sum, 4 * C)
            for g in range(NG):
                if g >= 2:
                    pe.wait_ge(kw_out, 2 * (g - 1))
                for c in range(C):
                    last = nc.tensor.matmul(ps_a[:, (g % 2) * 512:(g % 2 + 1) * 512],
                                            blkT[:, c, g * GB:(g + 1) * GB, :].rearrange("p b n -> p (b n)"),
                                            w_kwo[:, c, :], start=(c == 0), stop=(c == C - 1))
                last.then_inc(kw_mm, 1)
            pe.wait_ge(l_small, 3 * DMA)
            pe.wait_ge(c_step, 3)
            nc.tensor.matmul(ps_m[0:NG, 0:P], cs[:, :], ident, start=True, stop=True).then_inc(c_mm, 1)
            pe.wait_ge(c_step, 8)
            nc.tensor.matmul(ps_m[:, P:P + NG], cT[:, :], ident[0:NG, 0:NG], start=True, stop=True).then_inc(c_mm, 1)

            def spread_proj(k):
                pe.wait_ge(ra_ready, k + 1)
                for i in range(GT):
                    last = nc.tensor.matmul(ps_a[:, i * E:(i + 1) * E], ra[:, i * P:(i + 1) * P],
                                            bw[:, bass.ds(k, 1), :].rearrange("p o e -> p (o e)"),
                                            start=True, stop=True)
                    if i % 2:
                        last.then_inc(r_mm, 1)

            def transpose_y(k):
                pe.wait_ge(z_done, 2 * k + 2)
                for c in range(C):
                    for i in range(GT):
                        pe.wait_ge(y_done, GT * k + i + 1)
                        last = nc.tensor.transpose(ps_a[:, c * 512 + i * P:c * 512 + (i + 1) * P],
                                                   y[:, i, c * P:(c + 1) * P], ident)
                    last.then_inc(yt_mm, 1)

            def project_qk(k, w, done, h):
                for q in range(HW):
                    col = (h * HW + q) * 32
                    for c in range(C):
                        for b in range(TB):
                            dst = ps_a[32 * b:32 * b + 32, h * 512:(h + 1) * 512].rearrange(
                                "p (t n) -> p t n", t=GT)[:, :, q * S:(q + 1) * S]
                            rhs = yT[:, c, :].rearrange("p (t b s) -> p t b s", t=GT, b=TB)[:, :, b, :]
                            last = nc.tensor.matmul(dst, w[:, c, col:col + 32], rhs, start=(c == 0),
                                                    stop=(c == C - 1), tile_position=(0, 32 * b))
                last.then_inc(done, 1)

            def project_v(k, h):
                for i in (2 * h, 2 * h + 1):
                    for c in range(C):
                        last = nc.tensor.matmul(ps_a[:, i * E:(i + 1) * E], yT[:, c, i * P:(i + 1) * P], w_v[:, c, :],
                                                start=(c == 0), stop=(c == C - 1))
                last.then_inc(v_mm, 1)

            def quarter(k, i, h):
                if i == 0:
                    if h == 0:
                        pe.wait_ge(yt_out, C * k + C)
                    project_qk(k, w_q, q_mm, h)
                elif i == 1:
                    pe.wait_ge(q_out, 2 * k + h + 1)
                    project_qk(k, w_k, k_mm, h)
                elif i == 2:
                    pe.wait_ge(k_out, 2 * k + h + 1)
                    project_v(k, h)

            def scores(n, g, i, first=False):
                pe.wait_ge(k_in[i // 2], HG * DMA * (g + 1))
                pe.wait_ge(q_in[i // 2], TB * (g + 1))
                for h in range(2):
                    if not first:
                        pe.wait_ge(sc_out, 2 * n - 1 + h)
                    bank = ps_s[:, h * 512:(h + 1) * 512]
                    nc.tensor.matmul(bank, pick[0:3 * S, :], bias_t[0:3 * S, :, :].rearrange("p h k -> p (h k)"),
                                     start=True, stop=False)
                    for q in range(HW):
                        cols = slice((h * HW + q) * S, (h * HW + q + 1) * S)
                        last = nc.tensor.matmul(bank[:, q * P:(q + 1) * P],
                                                qbd[:, i, h * HW + q, :, :].rearrange("p b s -> p (b s)"), kbd[:, :, i, cols],
                                                start=False, stop=(q == HW - 1))
                    last.then_inc(sc_mm, 1)

            def transpose_probs(n, p, first=False):
                for h in range(2):
                    pe.wait_ge(sc_exp, 2 * n + h + 1)
                    if not first:
                        pe.wait_ge(pt_out, 2 * n - 1 + h)
                    for q in range(HW):
                        col = (h * HW + q) * P
                        last = nc.tensor.transpose(ps_t[:, col:col + P], sc[:, p, col:col + P], ident)
                    last.then_inc(pt_mm, 1)

            def probs_v(n, g, i):
                pe.wait_ge(v_in[i // 2], 16 * DMA * (g + 1))
                pe.wait_ge(pt_out, 2 * n + 2)
                for q in range(NQ):
                    for b in range(TB):
                        w = NQ * HD
                        last = nc.tensor.matmul(
                            ps_o[32 * b:32 * b + 32, q * 40:(q + 1) * 40], pT[:, q, 32 * b:32 * b + 32],
                            vbd[:, :, i, b * w + q * HD:b * w + (q + 1) * HD],
                            start=True, stop=True, tile_position=(0, 32 * b))
                last.then_inc(pv_mm, 1)

            def transpose_attn(n):
                pe.wait_ge(o_norm, n + 1)
                for c in range(C):
                    last = nc.tensor.transpose(ps_m[:, c * P:(c + 1) * P], on[:, c * P:(c + 1) * P], ident)
                last.then_inc(ot_mm, 1)

            def project_out(n):
                pe.wait_ge(ot_out, n + 1)
                for m in range(C):
                    for c in range(C):
                        last = nc.tensor.matmul(ps_m[:, E + m * P:E + (m + 1) * P], w_p[:, c, m * P:(m + 1) * P],
                                                oT[:, c, :], start=(c == 0), stop=(c == C - 1))
                last.then_inc(x1_mm, 1)

            pe.wait_ge(a_ready, 1)
            spread_proj(0)
            transpose_y(0)
            pe.wait_ge(l_attn, 5 * DMA)
            for i in range(3):
                for h in range(2):
                    quarter(0, i, h)
            pe.wait_ge(v_out, 2)
            spread_proj(1)
            pe.wait_ge(consts_cast, 3)
            scores(0, 0, 0, first=True)
            transpose_probs(0, 0, first=True)

            def tile_step(g, i, ahead, spread_ahead):
                n = GT * g + i
                last = not ahead and i == GT - 1
                if not last:
                    scores(n + 1, g + (i + 1) // GT, (i + 1) % GT)
                if ahead and i == 0:
                    transpose_y(g + 1)
                probs_v(n, g, i)
                if ahead:
                    quarter(g + 1, i, 0)
                if spread_ahead and i == 3:
                    pe.wait_ge(v_out, 2 * g + 4)
                    spread_proj(g + 2)
                transpose_attn(n)
                if ahead:
                    quarter(g + 1, i, 1)
                if not last:
                    transpose_probs(n + 1, (i + 1) % 2)
                project_out(n)

            with pe.Fori(0, NG - 2) as g:
                for i in range(GT):
                    tile_step(g, i, True, True)
            for g in (NG - 2, NG - 1):
                for i in range(GT):
                    tile_step(g, i, g == NG - 2, False)

            def gate(bank, w, col, rhs, first):
                for m in range(C):
                    for c in range(C):
                        last = nc.tensor.matmul(bank[:, m * B:(m + 1) * B], w[:, c, col + m * P:col + (m + 1) * P],
                                                rhs[:, c], start=(first and m == 0 and c == 0), stop=(c == C - 1),
                                                skip_group_check=True)
                return last

            def from_input(t, p):
                rhs = xf[:, :, bass.ds(t, 1), :].rearrange("p c o b -> p c (o b)")
                gate(gate_bank("r", p), w_ih, 0, rhs, True)
                gate(gate_bank("z", p), w_ih, E, rhs, True)
                gate(gate_bank("n", p), w_ih, 2 * E, rhs, True)

            def from_state(t, p):
                rhs = hT[:, 1 - p, :, :]
                gate(gate_bank("r", p), w_hh, 0, rhs, False).then_inc(g_r, 1)
                gate(gate_bank("z", p), w_hh, E, rhs, False).then_inc(g_z, 1)
                gate(ps_o[:, :], w_hh, 2 * E, rhs, True).then_inc(g_n, 1)

            def ffn(t, p):
                gate(ps_m[:, :], w_f, 0, hT[:, p, :, :], True).then_inc(f_mm, 1)

            pe.wait_ge(x1_out, C * (B // TB))
            pe.wait_ge(l_gru, 4 * DMA)
            pe.wait_ge(w_ready, 2)
            from_input(0, 0)
            from_state(0, 0)
            from_input(1, 1)

            def step(t, p, more, first=False):
                pe.wait_ge(h_done, C * t + C)
                from_state(t + 1, 1 - p)
                if not first:
                    pe.wait_ge(f_out, C * t)
                ffn(t, p)
                if more:
                    from_input(t + 2, p)

            step(0, 0, True, first=True)
            step(1, 1, True)
            with pe.Fori(1, (S - 2) // 2) as j:
                step(2 * j, 0, True)
                step(2 * j + 1, 1, True)
            step(S - 2, 0, False)
            pe.wait_ge(h_done, C * S)
            pe.wait_ge(f_out, C * (S - 1))
            ffn(S - 1, 1)


def kernel(x, cond_2048, L0_cond_rms_weight, L0_cond_Wk, L0_cond_Wo, L0_cond_ln_gamma, L0_cond_ln_beta,
           L0_attn_W_attn, L0_attn_b_attn, L0_attn_W_proj, L0_attn_b_proj, L0_cond2_W_ih, L0_cond2_W_hh,
           L0_cond2_b_ih, L0_cond2_b_hh, L0_ffn_weight, L0_ffn_scale_weight, L0_ffn_bias):
    import concourse.bacc as bacc
    from concourse.bass_utils import run_bass_kernel_spmd

    a = {k: np.asarray(v) for k, v in locals().items() if not k.startswith("b") or k.startswith("b_")}
    x, cond = a["x"], a["cond_2048"]
    wa, ba = a["L0_attn_W_attn"], a["L0_attn_b_attn"]

    def chunks(w):
        return w.reshape(C, P, -1).transpose(1, 0, 2)

    def qk_cols(w):
        return w.reshape(-1, NQ, HG, HD).transpose(0, 1, 3, 2).reshape(-1, E)

    def v_cols(w):
        return w.reshape(-1, NQ, HG, HD).transpose(0, 2, 1, 3).reshape(-1, E)

    def feature(v):
        return v.reshape(-1, P).T

    def qk_bias(v):
        t = v.reshape(NQ, HG, HD).transpose(2, 1, 0).reshape(HG * HD, NQ)
        return np.broadcast_to(t[None, :, :, None], (TB, HG * HD, NQ, S)).reshape(P, QT)

    vecs = np.concatenate([feature(a[n]) for n in (
        "L0_cond_ln_gamma", "L0_cond_ln_beta", "L0_attn_b_proj", "L0_ffn_bias", "L0_cond2_b_ih", "L0_cond2_b_hh")], 1)
    rows = np.stack([cond[1], a["L0_cond_rms_weight"], v_cols(ba[2 * E:])[0], a["L0_ffn_scale_weight"]])
    ins = {
        "x_tok": x.reshape(B * S // P, P, E),
        "x_feat": x.transpose(2, 1, 0).reshape(C, P, S, B),
        "cond_t": chunks(cond.T),
        "wkwo": np.concatenate([chunks(a["L0_cond_Wk"].T), chunks(a["L0_cond_Wo"].T)], 2),
        "wq": chunks(qk_cols(wa[:, 0:E])),
        "wk": chunks(qk_cols(wa[:, E:2 * E])),
        "wv": chunks(v_cols(wa[:, 2 * E:])),
        "wp": chunks(a["L0_attn_W_proj"]),
        "wih": chunks(a["L0_cond2_W_ih"]),
        "whh": chunks(a["L0_cond2_W_hh"]),
        "wf": chunks(a["L0_ffn_weight"].T),
        "vecs": vecs,
        "rows": np.broadcast_to(rows[None], (P, 4, E)),
        "bqk": np.stack([qk_bias(ba[0:E]), qk_bias(ba[E:2 * E])], 1),
        "consts": shape_constants(),
    }
    nc = bacc.Bacc("TRN2", target_bir_lowering=False, num_devices=1)
    arrays, args = {}, []
    for name, v in ins.items():
        v = np.ascontiguousarray(v)
        arrays["in_" + name] = v
        args.append(nc.dram_tensor("in_" + name, v.shape, mybir.dt.from_np(v.dtype), kind="ExternalInput").ap())
    out = nc.dram_tensor("out_feat", (S, P, C, B), F32, kind="ExternalOutput").ap()
    adaln_attn_gru_ffn(nc, *args, out)
    r = run_bass_kernel_spmd(nc, [arrays], core_ids=[0])
    got = r.results[0]["out_feat"]
    return got.transpose(3, 0, 2, 1).reshape(B, S, E)
```

```python
from contextlib import ExitStack

import numpy as np

import concourse.bass as bass
from concourse import mybir

ALU = mybir.AluOpType
ACT = mybir.ActivationFunctionType
AX_X = mybir.AxisListType.X
F32 = mybir.dt.float32
BF16 = mybir.dt.bfloat16
F32R = mybir.dt.float32r

B, S, E = 128, 32, 256
NH, HD = 32, 8
NBLK = 8
P = 128
C = E // P
TB = P // S
GT = 4
GB = GT * TB
NG = B // GB
HG = 4
NQ = NH // HG
HW = NQ // 2
GC = GT * P
QT = NQ * S
VT = TB * NQ * HD
SLOT = GT * QT
MASKED = -10000.0
EPS = 1e-6
BIG = float(2.0 ** 100)
SCALE = float(np.float32(1.0) / np.sqrt(np.float32(HD)))
PAIRS = S // 2
DMA = 16

V_GAMMA, V_BETA, V_BPROJ, V_FFNB, V_BIH, V_BHH = 0, 2, 4, 6, 8, 14
NVEC = 20
R_Q, R_RMS, R_BV, R_FSC = range(4)


def split_bf16(a):
    parts = []
    for _ in range(3):
        p = (a.view(np.uint32) & np.uint32(0xFFFF0000)).view(np.float32)
        parts.append(p)
        a = (a - p).astype(np.float32)
    return parts


def shape_constants():
    q, k = np.arange(S)[:, None], np.arange(S)[None, :]
    causal = k <= q
    slope = np.float32(2.0 ** (-(8.0 / NH)))
    alibi = np.where(causal, (k - q).astype(np.float32) * slope, np.float32(0)).astype(np.float32)
    parts = split_bf16(alibi)
    parts[0] = np.where(causal, parts[0], np.float32(BIG))
    bias = np.zeros((P, S), np.float32)
    bias[: 3 * S] = np.concatenate(parts, 0)
    pick = np.zeros((P, P), np.float32)
    for part in range(3):
        for r in range(S):
            pick[part * S + r, r::S] = 1.0
    floor = np.tile(np.where(causal, np.float32(3e38), np.float32(MASKED)), (TB, 1))
    spread = np.zeros((P, GC), np.float32)
    for b in range(GB):
        spread[b * NBLK:(b + 1) * NBLK, b * S:(b + 1) * S] = 1.0
    ident = np.eye(P, dtype=np.float32)
    return np.ascontiguousarray(np.concatenate([ident, pick, bias, floor, spread], 1).astype(np.float32))


K_ID, K_PICK, K_BIAS, K_FLOOR, K_SPREAD = 0, P, 2 * P, 2 * P + S, 2 * P + 2 * S
NCONST = 2 * P + 2 * S + GC


def adaln_attn_gru_ffn(nc, x_tok, x_feat, cond_t, wkwo, wq, wk, wv, wp, wih, whh, wf, vecs, rows, bqk, consts, out):
    ctx = ExitStack()
    with ctx:
        def sb(name, shape, dt=F32):
            return ctx.enter_context(nc.sbuf_tensor(name, shape, dt))

        def sem(name):
            return ctx.enter_context(nc.semaphore(name))

        xf = sb("xf", [P, C, NG, S, GB])
        xg = sb("xg", [P, GT, E])
        y = sb("y", [P, GT, E])
        yT = sb("yT", [P, C, GC])
        qn = sb("qn", [P, GT, QT])
        kn = sb("kn", [P, GT, QT])
        vn = sb("vn", [P, GT, E])
        vbd = sb("vbd", [P, HG + 1, GT, VT])
        sc = sb("sc", [P, 2, NH * S])
        pT = sb("pT", [P, NQ, P])
        mx = sb("mx", [P, 2, NH])
        rden = sb("rden", [P, NH])
        on = sb("on", [P, E])
        oT = sb("oT", [P, C, P])
        kw_sb = sb("kw_sb", [P, 2, E])
        junk = sb("junk", [P, 2, E])
        blkT = sb("blkT", [P, C, GB, NBLK])
        ssq = sb("ssq", [P, 1])
        dotq = sb("dotq", [P, 1])
        rinv = sb("rinv", [P, 1])
        cs = sb("cs", [P, 1])
        cT = sb("cT", [1, P])
        cmx = sb("cmx", [1, GB])
        csum = sb("csum", [1, GB])
        ra = sb("ra", [P, GC])
        st = sb("st", [P, GT, 6])
        mv = sb("mv", [P, GT, 2])
        rstd = sb("rstd", [P, GT])
        minus_half = sb("minus_half", [P, GT])
        carrier = sb("carrier", [P, 1])
        eps_t = sb("eps_t", [P, GT])
        wqr = sb("wqr", [P, E])
        w_kwo = sb("w_kwo", [P, C, 2 * E])
        w_q, w_k, w_v, w_p, w_f = (sb(n, [P, C, E]) for n in ("w_q", "w_k", "w_v", "w_p", "w_f"))
        w_ih = sb("w_ih", [P, C, 3 * E])
        w_hh = sb("w_hh", [P, C, 3 * E])
        vec = sb("vec", [P, NVEC])
        brz = sb("brz", [P, 4])
        row = sb("row", [P, 4, E])
        bq_t = sb("bq_t", [P, 2, QT])
        kst = sb("kst", [P, NCONST])
        pick = sb("pick", [P, P], BF16)
        bias_t = sb("bias_t", [P, HW * HG, S], BF16)
        hT = sb("hT", [P, 2, C, B])
        w_ih_r = [sb(f"w_ih_r{k}", [P, C, 3 * E], F32R) for k in range(2)]
        w_f_r = [sb(f"w_f_r{k}", [P, C, E], F32R) for k in range(2)]

        with ExitStack() as attention_only:
            qbd = attention_only.enter_context(nc.sbuf_tensor("qbd", [P, GT, NQ, TB, S], F32))
            kbd = attention_only.enter_context(nc.sbuf_tensor("kbd", [P, HG, GT, QT], F32))
        rg = sb("rg", [P, C, B])
        zg = sb("zg", [P, C, B])
        zc = sb("zc", [P, C, B])
        zh = sb("zh", [P, C, B])
        npre = sb("npre", [P, C, B])
        ng = sb("ng", [P, C, B])
        ost = sb("ost", [P, 2, C, 2 * B])
        x_r = [sb(f"x_r{k}", [P, 2, C, 2 * B], F32R) for k in range(2)]
        h_r = [sb(f"h_r{k}", [P, 2, C, 2 * B], F32R) for k in range(2)]

        ident = kst[:, K_ID:K_ID + P]
        floor_t = kst[:, K_FLOOR:K_FLOOR + S]
        spread = kst[:, K_SPREAD:K_SPREAD + GC]

        ps_s = ctx.enter_context(nc.psum_tensor("ps_s", [P, 1024], F32))
        ps_t = ctx.enter_context(nc.psum_tensor("ps_t", [P, 1024], F32))
        ps_o = ctx.enter_context(nc.psum_tensor("ps_o", [P, 512], F32))
        ps_m = ctx.enter_context(nc.psum_tensor("ps_m", [P, 512], F32))
        ps_a = ctx.enter_context(nc.psum_tensor("ps_a", [P, 1024], F32))

        l_xf0 = [sem(f"l_xf0_{k}") for k in range(3)]
        l_xf = sem("l_xf")
        l_xg = sem("l_xg")
        l_kwo = sem("l_kwo")
        l_small = sem("l_small")
        l_attn = sem("l_attn")
        l_gru = sem("l_gru")
        zeroed = sem("zeroed")
        consts_cast = sem("consts_cast")
        blk_sum = sem("blk_sum")
        wq_done = sem("wq_done")
        kw_mm = sem("kw_mm")
        kw_out = sem("kw_out")
        kw_red = sem("kw_red")
        c_mean = sem("c_mean")
        c_pow = sem("c_pow")
        c_dot = sem("c_dot")
        c_row = sem("c_row")
        c_max = sem("c_max")
        c_sub = sem("c_sub")
        c_exp = sem("c_exp")
        c_sum = sem("c_sum")
        c_inv = sem("c_inv")
        c_wt = sem("c_wt")
        c_col = sem("c_col")
        ra_ready = sem("ra_ready")
        r_mm = sem("r_mm")
        z_done = sem("z_done")
        bn_done = sem("bn_done")
        eps_added = sem("eps_added")
        y_done = sem("y_done")
        yt_mm = sem("yt_mm")
        yt_out = sem("yt_out")
        q_mm = sem("q_mm")
        k_mm = sem("k_mm")
        v_mm = sem("v_mm")
        q_out = sem("q_out")
        k_out = sem("k_out")
        v_out = sem("v_out")
        k_in = [sem("k_in0"), sem("k_in1")]
        q_in = [sem("q_in0"), sem("q_in1")]
        v_in = [sem("v_in0"), sem("v_in1")]
        sc_mm = sem("sc_mm")
        sc_out = sem("sc_out")
        sc_max = sem("sc_max")
        sc_sub = sem("sc_sub")
        sc_exp = sem("sc_exp")
        pt_mm = sem("pt_mm")
        pt_out = sem("pt_out")
        pv_mm = sem("pv_mm")
        den_inv = sem("den_inv")
        o_norm = sem("o_norm")
        ot_mm = sem("ot_mm")
        ot_out = sem("ot_out")
        x1_mm = sem("x1_mm")
        x1_out = sem("x1_out")
        w_ready = sem("w_ready")
        g_r = sem("g_r")
        g_z = sem("g_z")
        g_n = sem("g_n")
        s_r = sem("s_r")
        s_z = sem("s_z")
        zc_done = sem("zc_done")
        zh_done = sem("zh_done")
        rh_done = sem("rh_done")
        npre_done = sem("npre_done")
        n_done = sem("n_done")
        nz_done = sem("nz_done")
        h_done = sem("h_done")
        w_hi = sem("w_hi")
        w_lo = sem("w_lo")
        x_hi = sem("x_hi")
        x_lo = sem("x_lo")
        h_hi = sem("h_hi")
        h_lo = sem("h_lo")
        f_mm = sem("f_mm")
        f_out = sem("f_out")
        stored = [sem("stored0"), sem("stored1")]

        block = ctx.enter_context(nc.Block())

        def x_group(g):
            return x_tok[bass.ds(g * GT, GT), :, :].rearrange("t p e -> p t e")

        def gate_bank(which, q):
            return {"r": ps_s, "z": ps_t, "n": ps_a}[which][:, q * 512:(q + 1) * 512]

        def gate_part(which, q, e, m):
            return gate_bank(which, q)[:, (2 * m + e) * B:(2 * m + e + 1) * B]

        def step_pair(c, u):
            return xf[:, c, :, bass.ds(2 * u, 2), :].rearrange("p g t b -> p t g b")

        @block.sync
        def _(sp):
            sp.dma_start(xf[:, :, 0, :, :].rearrange("p c t b -> p c (t b)"), x_feat[0]).then_inc(l_xf0[0], DMA)
            sp.dma_start(w_kwo[:, :, :], wkwo).then_inc(l_kwo, DMA)
            sp.dma_start(row[:, :, :], rows).then_inc(l_small, DMA)
            sp.dma_start(vec[:, :], vecs).then_inc(l_small, DMA)
            sp.dma_start(kst[:, :], consts).then_inc(l_small, DMA)
            sp.dma_start(xg[:, :, :], x_group(0)).then_inc(l_xg, DMA)
            sp.dma_start(xf[:, :, 1, :, :].rearrange("p c t b -> p c (t b)"), x_feat[1]).then_inc(l_xf0[1], DMA)
            for dst, src in ((w_q, wq), (w_k, wk), (w_v, wv), (w_p, wp)):
                sp.dma_start(dst[:, :, :], src).then_inc(l_attn, DMA)
            sp.dma_start(bq_t[:, :, :], bqk).then_inc(l_attn, DMA)
            sp.dma_start(xf[:, :, 2, :, :].rearrange("p c t b -> p c (t b)"), x_feat[2]).then_inc(l_xf0[2], DMA)
            for dst, src in ((w_ih, wih), (w_hh, whh), (w_f, wf)):
                sp.dma_start(dst[:, :, :], src).then_inc(l_gru, DMA)
            sp.dma_start(hT[:, 1, :, :], cond_t).then_inc(l_gru, DMA)
            sp.wait_ge(zeroed, 3)

            def move_k(half):
                cols = slice(half * (SLOT // 2), (half + 1) * (SLOT // 2))
                for j in range(HG):
                    kflat = kn[:, :, :].rearrange("p t n -> p (t n)")
                    kd = kbd[:, j, :, :].rearrange("p t n -> p (t n)")
                    sp.dma_start(kd[j:P:HG, cols], kflat[j:P:HG, cols]).then_inc(k_in[half], DMA)

            def move_v(half):
                tiles = slice(2 * half, 2 * half + 2)
                for b in range(TB):
                    for h in range(HG):
                        w = NQ * HD
                        sp.dma_start(vbd[32 * h:32 * h + 32, h, tiles, b * w:(b + 1) * w],
                                     vn[32 * b:32 * b + 32, tiles, h * w:(h + 1) * w]).then_inc(v_in[half], DMA)

            sp.wait_ge(z_done, 2)
            sp.dma_start(xg[:, :, :], x_group(1)).then_inc(l_xg, DMA)
            sp.wait_ge(k_out, 2)
            move_k(0)
            move_k(1)
            sp.wait_ge(v_out, 2)
            move_v(0)
            move_v(1)

            def group_loads(g, norm_ahead, cond_ahead):
                if cond_ahead:
                    sp.wait_ge(blk_sum, C * g + 3 * C)
                    sp.dma_start(xf[:, :, bass.ds(g + 3, 1), :, :].rearrange("p c o t b -> p c (o t b)"),
                                 x_feat[bass.ds(g + 3, 1), :, :, :].rearrange("o p c n -> (o p) c n")
                                 ).then_inc(l_xf, DMA)
                if norm_ahead:
                    sp.wait_ge(z_done, 2 * g + 4)
                    sp.dma_start(xg[:, :, :], x_group(g + 2)).then_inc(l_xg, DMA)
                sp.wait_ge(k_out, 2 * g + 4)
                sp.wait_ge(sc_mm, 8 * g + 4)
                move_k(0)
                sp.wait_ge(sc_mm, 8 * g + 8)
                move_k(1)
                sp.wait_ge(v_out, 2 * g + 3)
                sp.wait_ge(pv_mm, 4 * g + 2)
                move_v(0)
                sp.wait_ge(pv_mm, 4 * g + 4)
                sp.wait_ge(v_out, 2 * g + 4)
                move_v(1)

            with sp.Fori(0, NG - 3) as g:
                group_loads(g, True, True)
            group_loads(NG - 3, True, False)
            group_loads(NG - 2, False, False)

            def store(u, q):
                sp.wait_ge(f_out, 2 * C * u + 2 * C)
                sp.dma_start(out[bass.ds(u, 1), :, :, :].rearrange("o p c n -> (o p) c n"),
                             ost[:, q, :, :]).then_inc(stored[q], DMA)

            with sp.Fori(0, PAIRS // 2) as j:
                store(2 * j, 0)
                store(2 * j + 1, 1)
            sp.wait_ge(stored[0], DMA * (PAIRS // 2))
            sp.wait_ge(stored[1], DMA * (PAIRS // 2))

        @block.gpsimd
        def _(pool):
            nc.gpsimd.memset(qbd[:, :, :, :, :], 0.0).then_inc(zeroed, 1)
            nc.gpsimd.memset(kbd[:, :, :, :], 0.0).then_inc(zeroed, 1)
            nc.gpsimd.memset(minus_half[:, :], -0.5).then_inc(eps_added, 1)
            nc.gpsimd.memset(eps_t[:, :], EPS).then_inc(eps_added, 1)
            pool.wait_ge(eps_added, 2)

            def inverse_std(k):
                pool.wait_ge(bn_done, 3 * k + 2)
                nc.gpsimd.tensor_tensor(rstd[:, :], mv[:, :, 1], eps_t[:, 0:GT], ALU.add).then_inc(eps_added, 1)
                pool.wait_ge(eps_added, k + 3)
                nc.gpsimd.tensor_tensor(rstd[:, :], rstd[:, :], minus_half[:, 0:GT], ALU.pow).then_inc(bn_done, 1)

            def inverse_rms(k):
                pool.wait_ge(c_mean, k + 1)
                nc.gpsimd.tensor_tensor(rinv[:, :], rinv[:, :], minus_half[:, 0:1], ALU.pow).then_inc(c_pow, 1)

            for k in range(2):
                inverse_rms(k)
                inverse_std(k)

            with pool.Fori(0, NG - 2) as g:
                inverse_rms(g + 2)
                inverse_std(g + 2)

        @block.scalar
        def _(act):
            def copy_out(dst, src):
                return nc.scalar.activation(dst, src, ACT.Copy)

            def cond_out(k, bank):
                act.wait_ge(kw_mm, k + 1)
                if not (isinstance(k, int) and k == 0):
                    act.wait_ge(kw_red, 2 * k)
                    act.wait_ge(r_mm, 2 * k)
                copy_out(kw_sb[:, :, :].rearrange("p a e -> p (a e)"), bank).then_inc(kw_out, 1)

            def cond_exp(k):
                act.wait_ge(c_sub, k + 1)
                nc.scalar.activation(cT[:, :], cT[:, :], ACT.Exp).then_inc(c_exp, 1)

            def transpose_out(k):
                for c in range(C):
                    act.wait_ge(yt_mm, C * k + c + 1)
                    nc.scalar.activation(yT[:, c, :], ps_a[:, c * 512:(c + 1) * 512], ACT.Identity,
                                         bias=vec[:, V_BETA + c:V_BETA + c + 1],
                                         scale=vec[:, V_GAMMA + c:V_GAMMA + c + 1]).then_inc(yt_out, 1)

            def place_q(k, half):
                act.wait_ge(q_out, 2 * k + 2)
                for b in range(TB):
                    part, tiles = slice(32 * b, 32 * b + 32), slice(2 * half, 2 * half + 2)
                    copy_out(qbd[part, tiles, :, b, :].rearrange("p t q s -> p (t q) s"),
                             qn[part, tiles, :].rearrange("p t (q s) -> p (t q) s", s=S)).then_inc(q_in[half], 1)

            def softmax_exp(n, p):
                for h in range(2):
                    act.wait_ge(sc_sub, 2 * n + h + 1)
                    part = sc[:, p, h * 512:(h + 1) * 512]
                    nc.scalar.activation(part, part, ACT.Exp).then_inc(sc_exp, 1)

            def probs_out(n):
                for h in range(2):
                    act.wait_ge(pt_mm, 2 * n + h + 1)
                    act.wait_ge(pv_mm, n)
                    copy_out(pT[:, h * HW:(h + 1) * HW, :].rearrange("p q n -> p (q n)"),
                             ps_t[:, h * 512:(h + 1) * 512]).then_inc(pt_out, 1)

            def attn_out(n):
                act.wait_ge(ot_mm, n + 1)
                copy_out(oT[:, :, :].rearrange("p c n -> p (c n)"), ps_m[:, 0:E]).then_inc(ot_out, 1)

            cond_out(0, ps_a[:, 0:512])
            cond_exp(0)
            cond_out(1, ps_m[:, :])
            act.wait_ge(l_small, 3 * DMA)
            transpose_out(0)
            cond_exp(1)
            act.wait_ge(zeroed, 3)
            place_q(0, 0)
            place_q(0, 1)
            softmax_exp(0, 0)
            probs_out(0)

            def tile_step(g, i, ahead, norm_ahead):
                n = GT * g + i
                last = not ahead and i == GT - 1
                if norm_ahead and i == 0:
                    cond_out(g + 2, ps_a[:, 0:512])
                if ahead and i == 0:
                    transpose_out(g + 1)
                if not last:
                    softmax_exp(n + 1, (i + 1) % 2)
                attn_out(n)
                if norm_ahead and i == 1:
                    cond_exp(g + 2)
                if not last:
                    probs_out(n + 1)
                if ahead and i == 1:
                    act.wait_ge(sc_mm, 8 * g + 4)
                    place_q(g + 1, 0)
                if ahead and i == 2:
                    act.wait_ge(sc_mm, 8 * g + 8)
                    place_q(g + 1, 1)

            with act.Fori(0, NG - 2) as g:
                for i in range(GT):
                    tile_step(g, i, True, True)
            for i in range(GT):
                tile_step(NG - 2, i, True, False)
            act.wait_ge(w_ready, 2)
            copy_out(w_ih_r[0][:, :, :], w_ih[:, :, :]).then_inc(w_hi, 1)
            copy_out(w_f_r[0][:, :, :], w_f[:, :, :]).then_inc(w_hi, 1)
            for i in range(GT):
                tile_step(NG - 1, i, False, False)

            def gates(t, q, e):
                for gate, dst, mm, done, b0 in (("r", rg, g_r, s_r, 0), ("z", zg, g_z, s_z, 2)):
                    act.wait_ge(mm, t + 1)
                    for c in range(C):
                        nc.scalar.activation(dst[:, c, :], gate_part(gate, q, e, c), ACT.Sigmoid,
                                             bias=brz[:, b0 + c:b0 + c + 1]).then_inc(done, 1)
                for c in range(C):
                    act.wait_ge(npre_done, C * t + c + 1)
                    nc.scalar.activation(ng[:, c, :], npre[:, c, :], ACT.Tanh).then_inc(n_done, 1)

            def round_state(t, q, e):
                act.wait_ge(h_done, C * t + C)
                copy_out(h_r[0][:, q, :, e * B:(e + 1) * B], hT[:, e, :, :]).then_inc(h_hi, 1)

            def round_input(u, q):
                for c in range(C):
                    copy_out(x_r[0][:, q, c, :].rearrange("p (t g b) -> p t g b", t=2, g=NG), step_pair(c, u)
                             ).then_inc(x_hi, 1)

            def pair(u, q, more):
                gates(2 * u, q, 0)
                round_state(2 * u, q, 0)
                if more:
                    round_input(u + 2, q)
                gates(2 * u + 1, q, 1)
                round_state(2 * u + 1, q, 1)

            act.wait_ge(x1_out, C * (B // TB))
            round_input(0, 0)
            round_input(1, 1)
            act.wait_ge(w_ready, 3)
            pair(0, 0, True)
            with act.Fori(0, (PAIRS - 4) // 2) as j:
                pair(2 * j + 1, 1, True)
                pair(2 * j + 2, 0, True)
            pair(PAIRS - 3, 1, True)
            pair(PAIRS - 2, 0, False)
            pair(PAIRS - 1, 1, False)

        @block.vector
        def _(dve):
            nc.vector.memset(vbd[:, 0:HG, :, :], 0.0)
            ones = vbd[:, HG, :, :].rearrange("p t (n d) -> p (t n) d", d=HD)
            nc.vector.memset(ones, 0.0).then_inc(consts_cast, 1)
            dve.wait_ge(consts_cast, 1)
            for h in range(HG):
                last = nc.vector.memset(ones[32 * h:32 * h + 32, :, h:h + 1], 1.0)
            last.then_inc(zeroed, 1)
            dve.wait_ge(l_small, 3 * DMA)
            nc.vector.tensor_copy(pick[:, :], kst[:, K_PICK:K_PICK + P]).then_inc(consts_cast, 1)
            nc.vector.tensor_copy(bias_t[:, :, :], kst[:, K_BIAS:K_BIAS + S].unsqueeze(1).to_broadcast(
                [P, HW * HG, S])).then_inc(consts_cast, 1)
            nc.vector.tensor_tensor(wqr[:, :], row[:, R_Q, :], row[:, R_RMS, :], ALU.mult).then_inc(wq_done, 1)

            def block_sums(k, loaded, n):
                dve.wait_ge(loaded, n)
                if not (isinstance(k, int) and k == 0):
                    dve.wait_ge(kw_mm, k)
                for c in range(C):
                    src = xf[:, c, bass.ds(k, 1), :, :].rearrange("p o (n w) b -> p (o n) b w", w=S // NBLK)
                    nc.vector.tensor_reduce(blkT[:, c, :, :].rearrange("p b n -> p n b"), src,
                                            axis=AX_X, op=ALU.add).then_inc(blk_sum, 1)

            def cond_sums(k):
                dve.wait_ge(kw_out, k + 1)
                keys = kw_sb[:, 0, :]
                nc.vector.tensor_tensor_reduce(out=junk[:, 0, :], in0=keys, in1=keys, scale=1.0, scalar=0.0,
                                               op0=ALU.mult, op1=ALU.add, accum_out=ssq[:, :]).then_inc(kw_red, 1)
                nc.vector.tensor_tensor_reduce(out=junk[:, 1, :], in0=keys, in1=wqr[:, :], scale=1.0, scalar=0.0,
                                               op0=ALU.mult, op1=ALU.add, accum_out=dotq[:, :]).then_inc(kw_red, 1)
                dve.wait_ge(kw_red, 2 * k + 2)
                nc.vector.tensor_scalar(rinv[:, :], ssq[:, :], 1.0 / E, EPS, ALU.mult, ALU.add).then_inc(c_mean, 1)

            def cond_scores(k):
                dve.wait_ge(c_pow, k + 1)
                nc.vector.tensor_tensor(cs[:, :], dotq[:, :], rinv[:, :], ALU.mult).then_inc(c_dot, 1)

            row_ps = ps_o[0:1, 320:320 + P].rearrange("g (b n) -> g b n", n=NBLK)
            cTv = cT[:, :].rearrange("g (b n) -> g b n", n=NBLK)

            def cond_shift(k):
                dve.wait_ge(c_row, k + 1)
                nc.vector.tensor_reduce(cmx[:, :], row_ps, axis=AX_X, op=ALU.max).then_inc(c_max, 1)
                dve.wait_ge(c_max, k + 1)
                nc.vector.tensor_tensor(cTv, row_ps, cmx[:, :].unsqueeze(2).to_broadcast([1, GB, NBLK]),
                                        ALU.subtract).then_inc(c_sub, 1)

            def cond_normalise(k):
                dve.wait_ge(c_exp, k + 1)
                nc.vector.tensor_reduce(csum[:, :], cTv, axis=AX_X, op=ALU.add).then_inc(c_sum, 1)
                dve.wait_ge(c_sum, k + 1)
                nc.vector.reciprocal(csum[:, :], csum[:, :]).then_inc(c_inv, 1)
                dve.wait_ge(c_inv, k + 1)
                nc.vector.tensor_tensor(cTv, cTv, csum[:, :].unsqueeze(2).to_broadcast([1, GB, NBLK]),
                                        ALU.mult).then_inc(c_wt, 1)

            def select_blocks(k):
                dve.wait_ge(c_col, k + 1)
                nc.vector.tensor_scalar(ra[:, :], spread, ps_o[:, 320 + P:321 + P], None, ALU.mult).then_inc(ra_ready, 1)

            def layer_norm(k):
                dve.wait_ge(l_xg, DMA * (k + 1))
                for h in range(2):
                    dve.wait_ge(r_mm, 2 * k + h + 1)
                    if h == 0:
                        dve.wait_ge(yt_mm, C * k)
                    nc.vector.tensor_tensor(y[:, 2 * h:2 * h + 2, :].rearrange("p t e -> p (t e)"),
                                            xg[:, 2 * h:2 * h + 2, :].rearrange("p t e -> p (t e)"),
                                            ps_a[:, h * 512:(h + 1) * 512], ALU.add).then_inc(z_done, 1)
                for i in range(GT):
                    dve.wait_ge(z_done, 2 * k + i // 2 + 1)
                    last = nc.vector.bn_stats(st[:, i, :], y[:, i, :])
                last.then_inc(bn_done, 1)
                dve.wait_ge(bn_done, 3 * k + 1)
                nc.vector.memset(carrier[:, :], 0.0)
                for i in range(GT):
                    last = nc.vector.bn_aggr(mv[:, i, :], st[:, i, :])
                last.then_inc(bn_done, 1)
                dve.wait_ge(bn_done, 3 * k + 2)
                dve.wait_ge(bn_done, 3 * k + 3)
                for i in range(GT):
                    nc.vector.tensor_scalar(y[:, i, :], y[:, i, :], mv[:, i, 0:1], rstd[:, i:i + 1],
                                            ALU.subtract, ALU.mult).then_inc(y_done, 1)

            def bank_as_tiles(h):
                return ps_a[:, h * 512:(h + 1) * 512].rearrange("p (t n) -> p t n", t=GT)

            def q_bias(k):
                w = HW * S
                for h in range(2):
                    dve.wait_ge(q_mm, 2 * k + h + 1)
                    if h == 0:
                        dve.wait_ge(q_in[1], TB * k)
                    nc.vector.scalar_tensor_tensor(
                        qn[:, :, h * w:(h + 1) * w], bank_as_tiles(h), SCALE,
                        bq_t[:, 0, h * w:(h + 1) * w].unsqueeze(1).to_broadcast([P, GT, w]),
                        ALU.mult, ALU.add).then_inc(q_out, 1)

            def k_bias(k):
                w = HW * S
                for h in range(2):
                    dve.wait_ge(k_mm, 2 * k + h + 1)
                    if h == 0:
                        dve.wait_ge(k_in[0], HG * DMA * k)
                        dve.wait_ge(k_in[1], HG * DMA * k)
                    nc.vector.tensor_tensor(
                        kn[:, :, h * w:(h + 1) * w], bank_as_tiles(h),
                        bq_t[:, 1, h * w:(h + 1) * w].unsqueeze(1).to_broadcast([P, GT, w]),
                        ALU.add).then_inc(k_out, 1)

            def v_bias(k):
                for h in range(2):
                    dve.wait_ge(v_mm, 2 * k + h + 1)
                    if h == 0:
                        dve.wait_ge(v_in[0], 16 * DMA * k)
                        dve.wait_ge(v_in[1], 16 * DMA * k)
                    nc.vector.tensor_tensor(
                        vn[:, 2 * h:2 * h + 2, :], ps_a[:, h * 512:(h + 1) * 512].rearrange("p (t e) -> p t e", t=2),
                        row[:, R_BV, :].unsqueeze(1).to_broadcast([P, 2, E]), ALU.add).then_inc(v_out, 1)

            def softmax_shift(n, p):
                halves = [(h, sc[:, p, h * 512:(h + 1) * 512].rearrange("p (h k) -> p h k", k=S),
                           mx[:, p, h * NH // 2:(h + 1) * NH // 2]) for h in range(2)]
                for h, part, _ in halves:
                    dve.wait_ge(sc_mm, 2 * n + h + 1)
                    nc.vector.tensor_tensor(part, ps_s[:, h * 512:(h + 1) * 512].rearrange("p (h k) -> p h k", k=S),
                                            floor_t.unsqueeze(1).to_broadcast([P, NH // 2, S]),
                                            ALU.min).then_inc(sc_out, 1)
                for h, part, m in halves:
                    dve.wait_ge(sc_out, 2 * n + h + 1)
                    nc.vector.tensor_reduce(m, part, axis=AX_X, op=ALU.max).then_inc(sc_max, 1)
                for h, part, m in halves:
                    dve.wait_ge(sc_max, 2 * n + h + 1)
                    nc.vector.tensor_tensor(part, part, m.unsqueeze(2).to_broadcast([P, NH // 2, S]),
                                            ALU.subtract).then_inc(sc_sub, 1)

            def normalise(n):
                dve.wait_ge(pv_mm, n + 1)
                o5 = ps_o[:, 0:NQ * 40].rearrange("p (q s d) -> p q s d", q=NQ, s=HG + 1)
                nc.vector.reciprocal(rden[:, :].rearrange("p (q s) -> p q s", s=HG), o5[:, :, HG, 0:HG]).then_inc(den_inv, 1)
                dve.wait_ge(den_inv, n + 1)
                nc.vector.tensor_tensor(
                    on[:, :].rearrange("p (q s d) -> p q s d", q=NQ, s=HG), o5[:, :, 0:HG, :],
                    rden[:, :].rearrange("p (q s) -> p q s", s=HG).unsqueeze(3).to_broadcast([P, NQ, HG, HD]),
                    ALU.mult).then_inc(o_norm, 1)

            def residual(n, g, i):
                dve.wait_ge(x1_mm, n + 1)
                for c in range(C):
                    xs = xf[:, c, bass.ds(g, 1), :, i * TB:(i + 1) * TB].rearrange("p o t b -> p (o b) t")
                    nc.vector.scalar_tensor_tensor(
                        xs, ps_m[:, E + c * P:E + (c + 1) * P].rearrange("p (b t) -> p b t", b=TB),
                        vec[:, V_BPROJ + c:V_BPROJ + c + 1], xs, ALU.add, ALU.add).then_inc(x1_out, 1)

            dve.wait_ge(wq_done, 1)
            block_sums(0, l_xf0[0], DMA)
            cond_sums(0)
            block_sums(1, l_xf0[1], DMA)
            cond_scores(0)
            cond_shift(0)
            cond_normalise(0)
            select_blocks(0)
            layer_norm(0)
            dve.wait_ge(l_attn, 5 * DMA)
            nc.vector.tensor_scalar(bq_t[:, 0, :], bq_t[:, 0, :], SCALE, None, ALU.mult).then_inc(w_ready, 1)
            cond_sums(1)
            cond_scores(1)
            dve.wait_ge(w_ready, 1)
            q_bias(0)
            cond_shift(1)
            k_bias(0)
            cond_normalise(1)
            v_bias(0)
            select_blocks(1)
            block_sums(2, l_xf0[2], DMA)
            softmax_shift(0, 0)
            layer_norm(1)

            dve.wait_ge(l_gru, 4 * DMA)
            nc.vector.tensor_tensor(w_f[:, :, :], w_f[:, :, :],
                                    row[:, R_FSC, :].unsqueeze(1).to_broadcast([P, C, E]), ALU.mult).then_inc(w_ready, 1)
            nc.vector.tensor_tensor(brz[:, :], vec[:, V_BIH:V_BIH + 4], vec[:, V_BHH:V_BHH + 4],
                                    ALU.add).then_inc(w_ready, 1)

            def tile_step(g, i, ahead, norm_ahead, cond_ahead):
                n = GT * g + i
                if ahead or i < GT - 1:
                    softmax_shift(n + 1, (i + 1) % 2)
                normalise(n)
                if ahead and i == 0:
                    q_bias(g + 1)
                if ahead and i == 1:
                    k_bias(g + 1)
                if ahead and i == 2:
                    v_bias(g + 1)
                if norm_ahead and i == 0:
                    cond_sums(g + 2)
                if norm_ahead and i == 1:
                    cond_shift(g + 2)
                if norm_ahead and i == 2:
                    select_blocks(g + 2)
                if norm_ahead and i == 3:
                    layer_norm(g + 2)
                residual(n, g, i)
                if cond_ahead and i == 2:
                    block_sums(g + 3, l_xf, DMA * (g + 1))
                if norm_ahead and i == 0:
                    cond_scores(g + 2)
                if norm_ahead and i == 1:
                    cond_normalise(g + 2)

            with dve.Fori(0, NG - 3) as g:
                for i in range(GT):
                    tile_step(g, i, True, True, True)
            for i in range(GT):
                tile_step(NG - 3, i, True, True, False)
            for i in range(GT):
                tile_step(NG - 2, i, True, False, False)
            for k, (w, w_r) in enumerate(((w_ih, w_ih_r), (w_f, w_f_r))):
                dve.wait_ge(w_hi, k + 1)
                nc.vector.tensor_tensor(w_r[1][:, :, :], w[:, :, :], w_r[0][:, :, :], ALU.subtract).then_inc(w_lo, 1)
            for i in range(GT):
                tile_step(NG - 1, i, False, False, False)

            def state(t, q, e):
                old, new = hT[:, 1 - e, :, :], hT[:, e, :, :]
                dve.wait_ge(g_n, t + 1)
                for c in range(C):
                    dve.wait_ge(s_r, C * t + c + 1)
                    nc.vector.scalar_tensor_tensor(rg[:, c, :], ps_o[:, c * B:(c + 1) * B],
                                                   vec[:, V_BHH + 4 + c:V_BHH + 5 + c], rg[:, c, :],
                                                   ALU.add, ALU.mult).then_inc(rh_done, 1)
                for c in range(C):
                    dve.wait_ge(rh_done, C * t + c + 1)
                    nc.vector.scalar_tensor_tensor(npre[:, c, :], gate_part("n", q, e, c),
                                                   vec[:, V_BIH + 4 + c:V_BIH + 5 + c], rg[:, c, :],
                                                   ALU.add, ALU.add).then_inc(npre_done, 1)
                dve.wait_ge(s_z, C * t + C)
                nc.vector.tensor_scalar(zc[:, :, :], zg[:, :, :], -1.0, 1.0, ALU.mult, ALU.add).then_inc(zc_done, 1)
                nc.vector.tensor_tensor(zh[:, :, :], zg[:, :, :], old, ALU.mult).then_inc(zh_done, 1)
                dve.wait_ge(zc_done, t + 1)
                for c in range(C):
                    dve.wait_ge(n_done, C * t + c + 1)
                    nc.vector.tensor_tensor(ng[:, c, :], ng[:, c, :], zc[:, c, :], ALU.mult).then_inc(nz_done, 1)
                dve.wait_ge(zh_done, t + 1)
                for c in range(C):
                    dve.wait_ge(nz_done, C * t + c + 1)
                    nc.vector.tensor_tensor(new[:, c, :], ng[:, c, :], zh[:, c, :], ALU.add).then_inc(h_done, 1)

            def rest_of_state(t, q, e):
                part = slice(e * B, (e + 1) * B)
                dve.wait_ge(h_hi, t + 1)
                nc.vector.tensor_tensor(h_r[1][:, q, :, part], hT[:, e, :, :], h_r[0][:, q, :, part],
                                        ALU.subtract).then_inc(h_lo, 1)

            def rest_of_input(u, q):
                for c in range(C):
                    dve.wait_ge(x_hi, C * u + c + 1)
                    lo, hi = (x[:, q, c, :].rearrange("p (t g b) -> p t g b", t=2, g=NG) for x in (x_r[1], x_r[0]))
                    nc.vector.tensor_tensor(lo, step_pair(c, u), hi, ALU.subtract).then_inc(x_lo, 1)

            def emit(u, q):
                dve.wait_ge(f_mm, u + 1)
                for c in range(C):
                    for e in range(2):
                        cols = slice((2 * c + e) * B, (2 * c + e + 1) * B)
                        nc.vector.scalar_tensor_tensor(
                            ost[:, q, c, e * B:(e + 1) * B].rearrange("p (g b) -> p g b", g=NG),
                            ps_m[:, cols].rearrange("p (g b) -> p g b", g=NG), vec[:, V_FFNB + c:V_FFNB + c + 1],
                            xf[:, c, :, bass.ds(2 * u + e, 1), :].rearrange("p g o b -> p g (o b)"),
                            ALU.add, ALU.add).then_inc(f_out, 1)

            def pair(u, q, more, stores=None):
                state(2 * u, q, 0)
                rest_of_state(2 * u, q, 0)
                if stores is not None:
                    dve.wait_ge(stored[1 - q], DMA * stores)
                if stores is not None or not isinstance(u, int) or u > 0:
                    emit(u - 1, 1 - q)
                state(2 * u + 1, q, 1)
                rest_of_state(2 * u + 1, q, 1)
                if more:
                    rest_of_input(u + 2, q)

            dve.wait_ge(x1_out, C * (B // TB))
            rest_of_input(0, 0)
            rest_of_input(1, 1)
            pair(0, 0, True)
            pair(1, 1, True)
            pair(2, 0, True)
            with dve.Fori(1, (PAIRS - 4) // 2) as j:
                pair(2 * j + 1, 1, True, stores=j)
                pair(2 * j + 2, 0, True, stores=j)
            pair(PAIRS - 3, 1, True, stores=PAIRS // 2 - 2)
            pair(PAIRS - 2, 0, False, stores=PAIRS // 2 - 2)
            pair(PAIRS - 1, 1, False, stores=PAIRS // 2 - 1)
            dve.wait_ge(stored[1], DMA * (PAIRS // 2 - 1))
            emit(PAIRS - 1, 1)

        @block.tensor
        def _(pe):
            def block_products(k, bank):
                pe.wait_ge(blk_sum, C * k + C)
                for c in range(C):
                    last = nc.tensor.matmul(bank, blkT[:, c, :, :].rearrange("p b n -> p (b n)"), w_kwo[:, c, :],
                                            start=(c == 0), stop=(c == C - 1))
                last.then_inc(kw_mm, 1)

            def cond_row(k):
                pe.wait_ge(c_dot, k + 1)
                nc.tensor.matmul(ps_o[0:1, 320:320 + P], cs[:, :], ident, start=True, stop=True).then_inc(c_row, 1)

            def cond_col(k):
                pe.wait_ge(c_wt, k + 1)
                nc.tensor.matmul(ps_o[:, 320 + P:321 + P], cT[:, :], ident[0:1, 0:1],
                                 start=True, stop=True).then_inc(c_col, 1)

            def spread_proj(k):
                pe.wait_ge(ra_ready, k + 1)
                for i in range(GT):
                    last = nc.tensor.matmul(ps_a[:, i * E:(i + 1) * E], ra[:, i * P:(i + 1) * P],
                                            kw_sb[:, 1, :],
                                            start=True, stop=True)
                    if i % 2:
                        last.then_inc(r_mm, 1)

            def transpose_y(k):
                pe.wait_ge(z_done, 2 * k + 2)
                for c in range(C):
                    for i in range(GT):
                        pe.wait_ge(y_done, GT * k + i + 1)
                        last = nc.tensor.transpose(ps_a[:, c * 512 + i * P:c * 512 + (i + 1) * P],
                                                   y[:, i, c * P:(c + 1) * P], ident)
                    last.then_inc(yt_mm, 1)

            def project_qk(k, w, done, h):
                for q in range(HW):
                    col = (h * HW + q) * 32
                    for c in range(C):
                        for b in range(TB):
                            dst = ps_a[32 * b:32 * b + 32, h * 512:(h + 1) * 512].rearrange(
                                "p (t n) -> p t n", t=GT)[:, :, q * S:(q + 1) * S]
                            rhs = yT[:, c, :].rearrange("p (t b s) -> p t b s", t=GT, b=TB)[:, :, b, :]
                            last = nc.tensor.matmul(dst, w[:, c, col:col + 32], rhs, start=(c == 0),
                                                    stop=(c == C - 1), tile_position=(0, 32 * b))
                last.then_inc(done, 1)

            def project_v(k, h):
                for i in (2 * h, 2 * h + 1):
                    for c in range(C):
                        last = nc.tensor.matmul(ps_a[:, i * E:(i + 1) * E], yT[:, c, i * P:(i + 1) * P], w_v[:, c, :],
                                                start=(c == 0), stop=(c == C - 1))
                last.then_inc(v_mm, 1)

            def quarter(k, i, h):
                if i == 0:
                    if h == 0:
                        pe.wait_ge(yt_out, C * k + C)
                    project_qk(k, w_q, q_mm, h)
                elif i == 1:
                    pe.wait_ge(q_out, 2 * k + h + 1)
                    project_qk(k, w_k, k_mm, h)
                elif i == 2:
                    pe.wait_ge(k_out, 2 * k + h + 1)
                    project_v(k, h)

            def scores(n, g, i, first=False):
                pe.wait_ge(k_in[i // 2], HG * DMA * (g + 1))
                pe.wait_ge(q_in[i // 2], TB * (g + 1))
                for h in range(2):
                    if not first:
                        pe.wait_ge(sc_out, 2 * n - 1 + h)
                    bank = ps_s[:, h * 512:(h + 1) * 512]
                    nc.tensor.matmul(bank, pick[0:3 * S, :], bias_t[0:3 * S, :, :].rearrange("p h k -> p (h k)"),
                                     start=True, stop=False)
                    for q in range(HW):
                        cols = slice((h * HW + q) * S, (h * HW + q + 1) * S)
                        last = nc.tensor.matmul(bank[:, q * P:(q + 1) * P],
                                                qbd[:, i, h * HW + q, :, :].rearrange("p b s -> p (b s)"), kbd[:, :, i, cols],
                                                start=False, stop=(q == HW - 1))
                    last.then_inc(sc_mm, 1)

            def transpose_probs(n, p, first=False):
                for h in range(2):
                    pe.wait_ge(sc_exp, 2 * n + h + 1)
                    if not first:
                        pe.wait_ge(pt_out, 2 * n - 1 + h)
                    for q in range(HW):
                        col = (h * HW + q) * P
                        last = nc.tensor.transpose(ps_t[:, col:col + P], sc[:, p, col:col + P], ident)
                    last.then_inc(pt_mm, 1)

            def probs_v(n, g, i):
                pe.wait_ge(v_in[i // 2], 16 * DMA * (g + 1))
                pe.wait_ge(pt_out, 2 * n + 2)
                for q in range(NQ):
                    for b in range(TB):
                        w = NQ * HD
                        last = nc.tensor.matmul(
                            ps_o[32 * b:32 * b + 32, q * 40:(q + 1) * 40], pT[:, q, 32 * b:32 * b + 32],
                            vbd[:, :, i, b * w + q * HD:b * w + (q + 1) * HD],
                            start=True, stop=True, tile_position=(0, 32 * b))
                last.then_inc(pv_mm, 1)

            def transpose_attn(n):
                pe.wait_ge(o_norm, n + 1)
                for c in range(C):
                    last = nc.tensor.transpose(ps_m[:, c * P:(c + 1) * P], on[:, c * P:(c + 1) * P], ident)
                last.then_inc(ot_mm, 1)

            def project_out(n):
                pe.wait_ge(ot_out, n + 1)
                for m in range(C):
                    for c in range(C):
                        last = nc.tensor.matmul(ps_m[:, E + m * P:E + (m + 1) * P], w_p[:, c, m * P:(m + 1) * P],
                                                oT[:, c, :], start=(c == 0), stop=(c == C - 1))
                last.then_inc(x1_mm, 1)

            pe.wait_ge(l_kwo, DMA)
            block_products(0, ps_a[:, 0:512])
            block_products(1, ps_m[:, :])
            pe.wait_ge(l_small, 3 * DMA)
            cond_row(0)
            cond_col(0)
            spread_proj(0)
            transpose_y(0)
            pe.wait_ge(l_attn, 5 * DMA)
            quarter(0, 0, 0)
            quarter(0, 0, 1)
            cond_row(1)
            quarter(0, 1, 0)
            quarter(0, 1, 1)
            cond_col(1)
            quarter(0, 2, 0)
            quarter(0, 2, 1)
            pe.wait_ge(consts_cast, 3)
            scores(0, 0, 0, first=True)
            pe.wait_ge(v_out, 2)
            spread_proj(1)
            pe.wait_ge(z_done, 4)
            block_products(2, ps_a[:, 0:512])
            transpose_probs(0, 0, first=True)

            def tile_step(g, i, ahead, norm_ahead, cond_ahead):
                n = GT * g + i
                last = not ahead and i == GT - 1
                if not last:
                    scores(n + 1, g + (i + 1) // GT, (i + 1) % GT)
                if norm_ahead and i == 0:
                    pe.wait_ge(kw_out, g + 3)
                if ahead and i == 0:
                    transpose_y(g + 1)
                if norm_ahead and i == 1:
                    cond_row(g + 2)
                if norm_ahead and i == 2:
                    cond_col(g + 2)
                if norm_ahead and i == 3:
                    pe.wait_ge(ra_ready, g + 3)
                probs_v(n, g, i)
                if ahead:
                    quarter(g + 1, i, 0)
                if norm_ahead and i == 3:
                    pe.wait_ge(v_out, 2 * g + 4)
                    spread_proj(g + 2)
                if ahead and i == 2:
                    quarter(g + 1, i, 1)
                transpose_attn(n)
                if ahead and i != 2:
                    quarter(g + 1, i, 1)
                if not last:
                    transpose_probs(n + 1, (i + 1) % 2)
                project_out(n)
                if cond_ahead and i == 3:
                    pe.wait_ge(z_done, 2 * g + 6)
                    block_products(g + 3, ps_a[:, 0:512])

            with pe.Fori(0, NG - 3) as g:
                for i in range(GT):
                    tile_step(g, i, True, True, True)
            for g in (NG - 3, NG - 2, NG - 1):
                for i in range(GT):
                    tile_step(g, i, g < NG - 1, g < NG - 2, False)

            def exact_product(bank, w_r, col, rhs_r):
                first = True
                for m in range(C):
                    for c in range(C):
                        for a, b in ((0, 0), (0, 1), (1, 0)):
                            last = nc.tensor.matmul(bank[:, m * 2 * B:(m + 1) * 2 * B],
                                                    w_r[a][:, c, col + m * P:col + (m + 1) * P], rhs_r[b][:, c, :],
                                                    start=first, stop=(c == C - 1 and a == 1), skip_group_check=True)
                            first = False
                return last

            def from_input(u, q, gates):
                for gate, col in gates:
                    exact_product(gate_bank(gate, q), w_ih_r, col, [x[:, q, :, :] for x in x_r])

            R_GATE, Z_GATE, N_GATE = ("r", 0), ("z", E), ("n", 2 * E)

            def from_state(q, e):
                old = hT[:, 1 - e, :, :]
                for which, done in (("r", g_r), (None, g_n), ("z", g_z)):
                    col = {"r": 0, "z": E, None: 2 * E}[which]
                    for c in range(C):
                        for m in range(C):
                            dst = gate_part(which, q, e, m) if which else ps_o[:, m * B:(m + 1) * B]
                            last = nc.tensor.matmul(dst, w_hh[:, c, col + m * P:col + (m + 1) * P], old[:, c, :],
                                                    start=(which is None and c == 0 and m == 0), stop=(c == C - 1),
                                                    skip_group_check=True)
                    last.then_inc(done, 1)

            def ffn(u, q):
                pe.wait_ge(h_lo, 2 * u + 2)
                exact_product(ps_m[:, :], w_f_r, 0, [h[:, q, :, :] for h in h_r]).then_inc(f_mm, 1)

            def pair(u, q, ahead, first=False):
                if not first:
                    pe.wait_ge(h_done, 2 * C * u)
                from_state(q, 0)
                if not first:
                    ffn(u - 1, 1 - q)
                if ahead:
                    pe.wait_ge(x_lo, C * u + 2 * C)
                    from_input(u + 1, 1 - q, (R_GATE,))
                pe.wait_ge(h_done, 2 * C * u + C)
                from_state(q, 1)
                if ahead:
                    from_input(u + 1, 1 - q, (Z_GATE, N_GATE))

            pe.wait_ge(x1_out, C * (B // TB))
            pe.wait_ge(l_gru, 4 * DMA)
            pe.wait_ge(w_ready, 3)
            pe.wait_ge(w_lo, 2)
            pe.wait_ge(x_lo, C)
            from_input(0, 0, (R_GATE, Z_GATE, N_GATE))
            pair(0, 0, True, first=True)
            with pe.Fori(0, (PAIRS - 2) // 2) as j:
                pair(2 * j + 1, 1, True)
                pair(2 * j + 2, 0, True)
            pair(PAIRS - 1, 1, False)
            ffn(PAIRS - 1, 1)


def kernel(x, cond_2048, L0_cond_rms_weight, L0_cond_Wk, L0_cond_Wo, L0_cond_ln_gamma, L0_cond_ln_beta,
           L0_attn_W_attn, L0_attn_b_attn, L0_attn_W_proj, L0_attn_b_proj, L0_cond2_W_ih, L0_cond2_W_hh,
           L0_cond2_b_ih, L0_cond2_b_hh, L0_ffn_weight, L0_ffn_scale_weight, L0_ffn_bias):
    import concourse.bacc as bacc
    from concourse.bass_utils import run_bass_kernel_spmd

    a = {k: np.asarray(v) for k, v in locals().items() if not k.startswith("b") or k.startswith("b_")}
    x, cond = a["x"], a["cond_2048"]
    wa, ba = a["L0_attn_W_attn"], a["L0_attn_b_attn"]

    def chunks(w):
        return w.reshape(C, P, -1).transpose(1, 0, 2)

    def qk_cols(w):
        return w.reshape(-1, NQ, HG, HD).transpose(0, 1, 3, 2).reshape(-1, E)

    def v_cols(w):
        return w.reshape(-1, NQ, HG, HD).transpose(0, 2, 1, 3).reshape(-1, E)

    def feature(v):
        return v.reshape(-1, P).T

    def qk_bias(v):
        t = v.reshape(NQ, HG, HD).transpose(2, 1, 0).reshape(HG * HD, NQ)
        return np.broadcast_to(t[None, :, :, None], (TB, HG * HD, NQ, S)).reshape(P, QT)

    vecs = np.concatenate([feature(a[n]) for n in (
        "L0_cond_ln_gamma", "L0_cond_ln_beta", "L0_attn_b_proj", "L0_ffn_bias", "L0_cond2_b_ih", "L0_cond2_b_hh")], 1)
    rows = np.stack([cond[1], a["L0_cond_rms_weight"], v_cols(ba[2 * E:])[0], a["L0_ffn_scale_weight"]])
    ins = {
        "x_tok": x.reshape(B * S // P, P, E),
        "x_feat": x.reshape(NG, GB, S, C, P).transpose(0, 4, 3, 2, 1).reshape(NG, P, C, S * GB),
        "cond_t": chunks(cond.T),
        "wkwo": np.concatenate([chunks(a["L0_cond_Wk"].T), chunks(a["L0_cond_Wo"].T)], 2),
        "wq": chunks(qk_cols(wa[:, 0:E])),
        "wk": chunks(qk_cols(wa[:, E:2 * E])),
        "wv": chunks(v_cols(wa[:, 2 * E:])),
        "wp": chunks(a["L0_attn_W_proj"]),
        "wih": chunks(a["L0_cond2_W_ih"]),
        "whh": chunks(a["L0_cond2_W_hh"]),
        "wf": chunks(a["L0_ffn_weight"].T),
        "vecs": vecs,
        "rows": np.broadcast_to(rows[None], (P, 4, E)),
        "bqk": np.stack([qk_bias(ba[0:E]), qk_bias(ba[E:2 * E])], 1),
        "consts": shape_constants(),
    }
    nc = bacc.Bacc("TRN2", target_bir_lowering=False, num_devices=1)
    arrays, args = {}, []
    for name, v in ins.items():
        v = np.ascontiguousarray(v)
        arrays["in_" + name] = v
        args.append(nc.dram_tensor("in_" + name, v.shape, mybir.dt.from_np(v.dtype), kind="ExternalInput").ap())
    out = nc.dram_tensor("out_feat", (PAIRS, P, C, 2 * B), F32, kind="ExternalOutput").ap()
    adaln_attn_gru_ffn(nc, *args, out)
    r = run_bass_kernel_spmd(nc, [arrays], core_ids=[0])
    got = r.results[0]["out_feat"]
    return got.reshape(PAIRS, P, C, 2, B).transpose(4, 0, 3, 2, 1).reshape(B, S, E)
```

```python
from contextlib import ExitStack

import numpy as np

import concourse.bass as bass
from concourse import mybir

ALU = mybir.AluOpType
ACT = mybir.ActivationFunctionType
AX_X = mybir.AxisListType.X
F32 = mybir.dt.float32
I32 = mybir.dt.int32
F32R = mybir.dt.float32r

B, S, E = 128, 32, 256
NH, HD = 32, 8
NBLK = 8
P = 128
C = E // P
TB = P // S
GT = 4
GB = GT * TB
NG = B // GB
HG = 4
NQ = NH // HG
HW = NQ // 2
GC = GT * P
GH = 2
TH = GT // GH
HT = TH * S
VW = NQ * HD
MASKED = -10000.0
EPS = 1e-6
SCALE = float(np.float32(1.0) / np.sqrt(np.float32(HD)))
PAIRS = S // 2
DMA = 16

V_GAMMA, V_BETA, V_BPROJ, V_FFNB, V_BIH, V_BHH, V_BQ, V_BK, V_BV = 0, 2, 4, 6, 8, 14, 20, 22, 24
NVEC = 26
R_Q, R_RMS, R_FSC = range(3)
NROW = 3


def shape_constants():
    q, k = np.arange(S)[:, None], np.arange(S)[None, :]
    causal = k <= q
    slope = 2.0 ** (-(8.0 / NH))
    fill = np.tile(np.where(causal, 0.0, MASKED - (k - q) * slope), (TB, 1))
    keep = np.tile(causal.astype(np.float32), (TB, 1))
    key = np.tile(np.exp((np.arange(S) - (S - 1)) * slope), P // S)[:, None]
    spread = np.zeros((P, GC), np.float32)
    for b in range(GB):
        spread[b * NBLK:(b + 1) * NBLK, b * S:(b + 1) * S] = 1.0
    return np.ascontiguousarray(np.concatenate([np.eye(P), fill, keep, key, spread], 1).astype(np.float32))


K_ID, K_FILL, K_KEEP, K_KEY, K_SPREAD = 0, P, P + S, P + 2 * S, P + 2 * S + 1
NCONST = K_SPREAD + GC


def adaln_attn_gru_ffn(nc, x_tok, x_feat, cond_t, wkwo, wqkv, wp, wih, whh, wf, vecs, rows, consts, q_dram, k_dram,
                       v_dram, out):
    ctx = ExitStack()
    with ctx:
        def sb(name, shape, dt=F32):
            return ctx.enter_context(nc.sbuf_tensor(name, shape, dt))

        def sem(name):
            return ctx.enter_context(nc.semaphore(name))

        xf = sb("xf", [P, C, NG, S, GB])
        xg = sb("xg", [P, GT, E])
        y = sb("y", [P, GT, E])
        yT = sb("yT", [P, C, GC])
        yT_r = [sb(f"yT_r{k}", [P, C, GC], F32R) for k in range(2)]
        qn = sb("qn", [P, C, GH * TB, HT])
        kn = sb("kn", [P, C, GH * TB, HT])
        vn = sb("vn", [P, GH, HG, TH * VW])
        vbd = sb("vbd", [P, HG + 1, GH, TB, TH * VW])
        sc = sb("sc", [P, 2, NH * S])
        pT = sb("pT", [P, NQ, P])
        mx = sb("mx", [P, 2, NH])
        rden = sb("rden", [P, NH])
        on = sb("on", [P, E])
        oT = sb("oT", [P, C, P])
        kw_sb = sb("kw_sb", [P, 2, E])
        junk = sb("junk", [P, 2, E])
        blkT = sb("blkT", [P, C, GB, NBLK])
        ssq = sb("ssq", [P, 1])
        dotq = sb("dotq", [P, 1])
        rinv = sb("rinv", [P, 1])
        cs = sb("cs", [P, 1])
        cT = sb("cT", [1, P])
        cmx = sb("cmx", [1, GB])
        csum = sb("csum", [1, GB])
        ra = sb("ra", [P, GC])
        st = sb("st", [P, GT, 6])
        mv = sb("mv", [P, GT, 2])
        rstd = sb("rstd", [P, GT])
        centre = sb("centre", [P, GT])
        minus_half = sb("minus_half", [P, GT])
        minus_one = sb("minus_one", [P, GT])
        carrier = sb("carrier", [P, 3])
        eps_t = sb("eps_t", [P, GT])
        wqr = sb("wqr", [P, E])
        w_kwo = sb("w_kwo", [P, C, 2 * E])
        w_p, w_f = (sb(n, [P, C, E]) for n in ("w_p", "w_f"))
        w_ih = sb("w_ih", [P, C, 3 * E])
        w_hh = sb("w_hh", [P, C, 3 * E])
        vec = sb("vec", [P, NVEC])
        brz = sb("brz", [P, 4])
        row = sb("row", [P, NROW, E])
        bq = sb("bq", [P, C])
        b_out = sb("b_out", [P, C])
        kst = sb("kst", [P, NCONST])
        masked = sb("masked", [P, NH * S])
        hT = sb("hT", [P, 2, C, B])
        w_qkv_r = [sb(f"w_qkv_r{k}", [P, C, 3 * E], F32R) for k in range(2)]
        with ExitStack() as first_group_only:
            w_qkv = first_group_only.enter_context(nc.sbuf_tensor("w_qkv", [P, C, 3 * E], F32))
        w_ih_r = [sb(f"w_ih_r{k}", [P, C, 3 * E], F32R) for k in range(2)]
        w_f_r = [sb(f"w_f_r{k}", [P, C, E], F32R) for k in range(2)]

        with ExitStack() as attention_only:
            qbd = attention_only.enter_context(nc.sbuf_tensor("qbd", [P, GH, NQ, TB, HT], F32))
            kbd = attention_only.enter_context(nc.sbuf_tensor("kbd", [P, HG, GH, NQ, HT], F32))
        rg = sb("rg", [P, C, B])
        zg = sb("zg", [P, C, B])
        zc = sb("zc", [P, C, B])
        zh = sb("zh", [P, C, B])
        npre = sb("npre", [P, C, B])
        ng = sb("ng", [P, C, B])
        ost = sb("ost", [P, 2, C, 2 * B])
        x_r = [sb(f"x_r{k}", [P, 2, C, 2 * B], F32R) for k in range(2)]
        h_r = [sb(f"h_r{k}", [P, 2, C, 2 * B], F32R) for k in range(2)]

        ident = kst[:, K_ID:K_ID + P]
        keep = kst[:, K_KEEP:K_KEEP + S].bitcast(I32)
        key_factor = kst[:, K_KEY:K_KEY + 1]
        spread = kst[:, K_SPREAD:K_SPREAD + GC]

        ps_s = ctx.enter_context(nc.psum_tensor("ps_s", [P, 1024], F32))
        ps_t = ctx.enter_context(nc.psum_tensor("ps_t", [P, 1024], F32))
        ps_o = ctx.enter_context(nc.psum_tensor("ps_o", [P, 512], F32))
        ps_m = ctx.enter_context(nc.psum_tensor("ps_m", [P, 512], F32))
        ps_a = ctx.enter_context(nc.psum_tensor("ps_a", [P, 1024], F32))

        l_xf0 = [sem(f"l_xf0_{k}") for k in range(3)]
        l_xf = sem("l_xf")
        l_xg = sem("l_xg")
        l_kwo = sem("l_kwo")
        l_small = sem("l_small")
        l_attn = sem("l_attn")
        l_gru = sem("l_gru")
        warm_zeros = sem("warm_zeros")
        zeroed = sem("zeroed")
        filled = sem("filled")
        blk_sum = sem("blk_sum")
        wq_done = sem("wq_done")
        kw_mm = sem("kw_mm")
        kw_out = sem("kw_out")
        kw_red = sem("kw_red")
        c_mean = sem("c_mean")
        c_pow = sem("c_pow")
        c_dot = sem("c_dot")
        c_row = sem("c_row")
        c_max = sem("c_max")
        c_sub = sem("c_sub")
        c_exp = sem("c_exp")
        c_sum = sem("c_sum")
        c_inv = sem("c_inv")
        c_wt = sem("c_wt")
        c_col = sem("c_col")
        ra_ready = sem("ra_ready")
        r_mm = sem("r_mm")
        z_done = sem("z_done")
        bn_done = sem("bn_done")
        pool_consts = sem("pool_consts")
        eps_added = sem("eps_added")
        std_done = sem("std_done")
        mean_neg = sem("mean_neg")
        centre_done = sem("centre_done")
        y_done = sem("y_done")
        yt_mm = sem("yt_mm")
        yt_out = sem("yt_out")
        yt_hi = sem("yt_hi")
        yt_lo = sem("yt_lo")
        wqkv_hi = sem("wqkv_hi")
        wqkv_lo = sem("wqkv_lo")
        q_saved = sem("q_saved")
        k_saved = sem("k_saved")
        v_saved = sem("v_saved")
        bv_mm = sem("bv_mm")
        b_out_done = sem("b_out_done")
        q_mm = sem("q_mm")
        k_mm = sem("k_mm")
        v_mm = sem("v_mm")
        q_out = sem("q_out")
        k_out = sem("k_out")
        v_out = sem("v_out")
        k_in = [sem("k_in0"), sem("k_in1")]
        q_in = [sem("q_in0"), sem("q_in1")]
        v_in = [sem("v_in0"), sem("v_in1")]
        sc_mm = sem("sc_mm")
        sc_out = sem("sc_out")
        sc_max = sem("sc_max")
        sc_sub = sem("sc_sub")
        sc_exp = sem("sc_exp")
        pt_mm = sem("pt_mm")
        pt_out = sem("pt_out")
        pv_mm = sem("pv_mm")
        den_inv = sem("den_inv")
        o_norm = sem("o_norm")
        ot_mm = sem("ot_mm")
        ot_out = sem("ot_out")
        x1_mm = sem("x1_mm")
        x1_out = sem("x1_out")
        w_ready = sem("w_ready")
        g_r = sem("g_r")
        g_z = sem("g_z")
        g_n = sem("g_n")
        s_r = sem("s_r")
        s_z = sem("s_z")
        zc_done = sem("zc_done")
        zh_done = sem("zh_done")
        rh_done = sem("rh_done")
        npre_done = sem("npre_done")
        n_done = sem("n_done")
        nz_done = sem("nz_done")
        h_done = sem("h_done")
        w_hi = sem("w_hi")
        w_lo = sem("w_lo")
        x_hi = sem("x_hi")
        x_lo = sem("x_lo")
        h_hi = sem("h_hi")
        h_lo = sem("h_lo")
        f_mm = sem("f_mm")
        f_out = sem("f_out")
        stored = [sem("stored0"), sem("stored1")]

        block = ctx.enter_context(nc.Block())

        def x_group(g):
            return x_tok[bass.ds(g * GT, GT), :, :].rearrange("t p e -> p t e")

        def gate_bank(which, q):
            return {"r": ps_s, "z": ps_t, "n": ps_a}[which][:, q * 512:(q + 1) * 512]

        def gate_part(which, q, e, m):
            return gate_bank(which, q)[:, (2 * m + e) * B:(2 * m + e + 1) * B]

        def step_pair(c, u):
            return xf[:, c, :, bass.ds(2 * u, 2), :].rearrange("p g t b -> p t g b")

        @block.sync
        def _(sp):
            sp.dma_start(xf[:, :, 0, :, :].rearrange("p c t b -> p c (t b)"), x_feat[0]).then_inc(l_xf0[0], DMA)
            sp.dma_start(w_kwo[:, :, :], wkwo).then_inc(l_kwo, DMA)
            sp.dma_start(row[:, :, :], rows).then_inc(l_small, DMA)
            sp.dma_start(vec[:, :], vecs).then_inc(l_small, DMA)
            sp.dma_start(kst[:, :], consts).then_inc(l_small, DMA)
            sp.dma_start(xg[:, :, :], x_group(0)).then_inc(l_xg, DMA)
            sp.dma_start(w_qkv[:, :, :], wqkv).then_inc(l_attn, DMA)
            sp.dma_start(xf[:, :, 1, :, :].rearrange("p c t b -> p c (t b)"), x_feat[1]).then_inc(l_xf0[1], DMA)
            sp.dma_start(w_p[:, :, :], wp).then_inc(l_attn, DMA)
            sp.dma_start(xf[:, :, 2, :, :].rearrange("p c t b -> p c (t b)"), x_feat[2]).then_inc(l_xf0[2], DMA)
            for dst, src in ((w_ih, wih), (w_hh, whh), (w_f, wf)):
                sp.dma_start(dst[:, :, :], src).then_inc(l_gru, DMA)
            sp.dma_start(hT[:, 1, :, :], cond_t).then_inc(l_gru, DMA)
            sp.wait_ge(zeroed, 4)

            def save_qk(dram, src, k, saved, chunks=range(C)):
                for m in chunks:
                    sp.dma_start(dram[bass.ds(k, 1), :, m * P:(m + 1) * P, :].rearrange("o x p n -> p (o x) n"),
                                 src[:, m, :, :]).then_inc(saved, DMA)

            def load_q(k, half):
                for b in range(TB):
                    sp.dma_start(qbd[32 * b:32 * b + 32, half, :, b, :],
                                 q_dram[bass.ds(k, 1), half * TB + b, :, :].rearrange(
                                     "o (r q) n -> (o r) q n", q=NQ)).then_inc(q_in[half], DMA)

            def load_k(k, half):
                for j in range(HG):
                    rows = k_dram[bass.ds(k, 1), half * TB:(half + 1) * TB, :, :].rearrange(
                        "o b (d j q) n -> (o b d) j (q n)", j=HG, q=NQ)
                    sp.dma_start(kbd[j:P:HG, j, half, :, :].rearrange("p q n -> p (q n)"),
                                 rows[:, j, :]).then_inc(k_in[half], DMA)

            def save_v(k, half):
                sp.dma_start(v_dram[bass.ds(k, 1), half, :, :, :].rearrange("o h p n -> p (o h) n"),
                             vn[:, half, :, :]).then_inc(v_saved, DMA)

            def load_v(k, half):
                for h in range(HG):
                    sp.dma_start(vbd[32 * h:32 * h + 32, h, half, :, :],
                                 v_dram[bass.ds(k, 1), half, h, :, :].rearrange("o (b s) n -> s (o b) n", b=TB)
                                 ).then_inc(v_in[half], DMA)

            sp.wait_ge(z_done, 2)
            sp.dma_start(xg[:, :, :], x_group(1)).then_inc(l_xg, DMA)
            sp.wait_ge(q_out, C)
            save_qk(q_dram, qn, 0, q_saved)
            for m in range(C):
                sp.wait_ge(k_out, m + 1)
                save_qk(k_dram, kn, 0, k_saved, (m,))
            sp.wait_ge(q_saved, C * DMA)
            load_q(0, 0)
            sp.wait_ge(k_saved, C * DMA)
            load_k(0, 0)
            sp.wait_ge(v_out, 2)
            save_v(0, 0)
            save_v(0, 1)
            sp.wait_ge(v_saved, 2 * DMA)
            load_v(0, 0)
            load_q(0, 1)
            load_k(0, 1)
            load_v(0, 1)

            def group_loads(g, norm_ahead, cond_ahead):
                if cond_ahead:
                    sp.wait_ge(blk_sum, C * g + 3 * C)
                    sp.dma_start(xf[:, :, bass.ds(g + 3, 1), :, :].rearrange("p c o t b -> p c (o t b)"),
                                 x_feat[bass.ds(g + 3, 1), :, :, :].rearrange("o p c n -> (o p) c n")
                                 ).then_inc(l_xf, DMA)
                if norm_ahead:
                    sp.wait_ge(z_done, 2 * g + 4)
                    sp.dma_start(xg[:, :, :], x_group(g + 2)).then_inc(l_xg, DMA)
                sp.wait_ge(q_out, 2 * g + 4)
                save_qk(q_dram, qn, g + 1, q_saved)
                sp.wait_ge(sc_mm, 8 * g + 4)
                sp.wait_ge(q_saved, C * DMA * g + 2 * C * DMA)
                load_q(g + 1, 0)
                sp.wait_ge(k_out, 2 * g + 3)
                save_qk(k_dram, kn, g + 1, k_saved, (0,))
                sp.wait_ge(k_out, 2 * g + 4)
                save_qk(k_dram, kn, g + 1, k_saved, (1,))
                sp.wait_ge(k_saved, C * DMA * g + 2 * C * DMA)
                load_k(g + 1, 0)
                sp.wait_ge(sc_mm, 8 * g + 8)
                load_k(g + 1, 1)
                load_q(g + 1, 1)
                sp.wait_ge(v_out, 2 * g + 3)
                save_v(g + 1, 0)
                sp.wait_ge(v_saved, 2 * DMA * g + 3 * DMA)
                sp.wait_ge(pv_mm, 4 * g + 2)
                load_v(g + 1, 0)
                sp.wait_ge(v_out, 2 * g + 4)
                save_v(g + 1, 1)
                sp.wait_ge(pv_mm, 4 * g + 4)
                sp.wait_ge(v_saved, 2 * DMA * g + 4 * DMA)
                load_v(g + 1, 1)

            with sp.Fori(0, NG - 3) as g:
                group_loads(g, True, True)
            group_loads(NG - 3, True, False)
            group_loads(NG - 2, False, False)

            def store(u, q):
                sp.wait_ge(f_out, 2 * C * u + 2 * C)
                sp.dma_start(out[bass.ds(u, 1), :, :, :].rearrange("o p c n -> (o p) c n"),
                             ost[:, q, :, :]).then_inc(stored[q], DMA)

            with sp.Fori(0, PAIRS // 2) as j:
                store(2 * j, 0)
                store(2 * j + 1, 1)
            sp.wait_ge(stored[0], DMA * (PAIRS // 2))
            sp.wait_ge(stored[1], DMA * (PAIRS // 2))

        @block.gpsimd
        def _(pool):
            nc.gpsimd.memset(oT[:, :, :], 0.0).then_inc(warm_zeros, 1)
            nc.gpsimd.memset(minus_half[:, :], -0.5).then_inc(pool_consts, 1)
            nc.gpsimd.memset(minus_one[:, :], -1.0).then_inc(pool_consts, 1)
            nc.gpsimd.memset(eps_t[:, :], EPS).then_inc(pool_consts, 1)
            nc.gpsimd.memset(qbd[:, :, :, :, :], 0.0).then_inc(zeroed, 1)
            nc.gpsimd.memset(kbd[:, :, :, :, :], 0.0).then_inc(zeroed, 1)
            pool.wait_ge(pool_consts, 3)

            def inverse_std(k):
                pool.wait_ge(bn_done, 2 * k + 2)
                pool.wait_ge(y_done, GT * k)
                nc.gpsimd.tensor_tensor(rstd[:, :], mv[:, :, 1], eps_t[:, :], ALU.add).then_inc(eps_added, 1)
                nc.gpsimd.tensor_tensor(centre[:, :], mv[:, :, 0], minus_one[:, :], ALU.mult).then_inc(mean_neg, 1)
                pool.wait_ge(eps_added, k + 1)
                nc.gpsimd.tensor_tensor(rstd[:, :], rstd[:, :], minus_half[:, :], ALU.pow).then_inc(std_done, 1)
                pool.wait_ge(mean_neg, k + 1)
                pool.wait_ge(std_done, k + 1)
                nc.gpsimd.tensor_tensor(centre[:, :], centre[:, :], rstd[:, :], ALU.mult).then_inc(centre_done, 1)

            def inverse_rms(k):
                pool.wait_ge(c_mean, k + 1)
                nc.gpsimd.tensor_tensor(rinv[:, :], rinv[:, :], minus_half[:, 0:1], ALU.pow).then_inc(c_pow, 1)

            def rest_of_y(k):
                for c in range(C):
                    pool.wait_ge(yt_hi, C * k + c + 1)
                    pool.wait_ge(yt_out, C * k + c + 1)
                    nc.gpsimd.tensor_tensor(yT_r[1][:, c, :], yT[:, c, :], yT_r[0][:, c, :],
                                            ALU.subtract).then_inc(yt_lo, 1)

            inverse_rms(0)
            nc.gpsimd.memset(vbd[:, 0:HG, :, :, :], 0.0).then_inc(zeroed, 1)
            inverse_std(0)
            rest_of_y(0)
            inverse_rms(1)
            inverse_std(1)
            with pool.Fori(0, NG - 2) as g:
                rest_of_y(g + 1)
                inverse_rms(g + 2)
                inverse_std(g + 2)
            rest_of_y(NG - 1)

        @block.scalar
        def _(act):
            def copy_out(dst, src):
                return nc.scalar.activation(dst, src, ACT.Copy)

            def cond_out(k, bank, first=False):
                act.wait_ge(kw_mm, k + 1)
                if not first:
                    act.wait_ge(kw_red, 2 * k)
                    act.wait_ge(r_mm, 2 * k)
                copy_out(kw_sb[:, :, :].rearrange("p a e -> p (a e)"), bank).then_inc(kw_out, 1)

            def cond_exp(k):
                act.wait_ge(c_sub, k + 1)
                nc.scalar.activation(cT[:, :], cT[:, :], ACT.Exp).then_inc(c_exp, 1)

            def normalise_tokens(k, tiles=range(GT)):
                act.wait_ge(std_done, k + 1)
                act.wait_ge(centre_done, k + 1)
                for i in tiles:
                    nc.scalar.activation(y[:, i, :], y[:, i, :], ACT.Identity, bias=centre[:, i:i + 1],
                                         scale=rstd[:, i:i + 1]).then_inc(y_done, 1)

            def transpose_out(k):
                for c in range(C):
                    act.wait_ge(yt_mm, C * k + c + 1)
                    for dst, out_sem in ((yT_r[0], yt_hi), (yT, yt_out)):
                        nc.scalar.activation(dst[:, c, :], ps_a[:, c * 512:(c + 1) * 512], ACT.Identity,
                                             bias=vec[:, V_BETA + c:V_BETA + c + 1],
                                             scale=vec[:, V_GAMMA + c:V_GAMMA + c + 1]).then_inc(out_sem, 1)

            def feature_out(k, m, dst, order, done, out_sem, saved, bias, scale):
                act.wait_ge(done, C * k + m + 1)
                if m == 0:
                    act.wait_ge(saved, C * DMA * k)
                for half in range(GH):
                    src = ps_a[:, m * GC + half * TH * P:m * GC + (half + 1) * TH * P]
                    last = nc.scalar.activation(
                        dst[:, m, half * TB:(half + 1) * TB, :].rearrange(f"p b {order} -> p b t s", t=TH),
                        src.rearrange("p (t b s) -> p b t s", t=TH, b=TB), ACT.Identity,
                        bias=bias[:, m:m + 1], scale=scale)
                last.then_inc(out_sem, 1)

            def q_chunk(k, m):
                feature_out(k, m, qn, "(s t)", q_mm, q_out, q_saved, bq, SCALE)

            def k_chunk(k, m):
                feature_out(k, m, kn, "(t s)", k_mm, k_out, k_saved, vec[:, V_BK:V_BK + C], 1.0)

            def v_half(k, half):
                act.wait_ge(v_mm, 2 * k + half + 1)
                if half == 0:
                    act.wait_ge(v_saved, 2 * DMA * k)
                nc.scalar.activation(vn[:, half, :, :].rearrange("p h (t w) -> p t h w", t=TH),
                                     ps_a[:, half * 512:(half + 1) * 512].rearrange("p (t h w) -> p t h w", t=TH, h=HG),
                                     ACT.Identity, scale=key_factor).then_inc(v_out, 1)

            def softmax_exp(n, p):
                for h in range(2):
                    act.wait_ge(sc_sub, 2 * n + h + 1)
                    part = sc[:, p, h * 512:(h + 1) * 512]
                    nc.scalar.activation(part, part, ACT.Exp).then_inc(sc_exp, 1)

            def probs_out(n):
                for h in range(2):
                    act.wait_ge(pt_mm, 2 * n + h + 1)
                    act.wait_ge(pv_mm, n)
                    copy_out(pT[:, h * HW:(h + 1) * HW, :].rearrange("p q n -> p (q n)"),
                             ps_t[:, h * 512:(h + 1) * 512]).then_inc(pt_out, 1)

            def attn_out(n):
                act.wait_ge(ot_mm, n + 1)
                copy_out(oT[:, :, :].rearrange("p c n -> p (c n)"), ps_m[:, 0:E]).then_inc(ot_out, 1)

            cond_out(0, ps_a[:, 0:512], first=True)
            cond_exp(0)
            act.wait_ge(l_attn, 2 * DMA)
            for m in range(3):
                cols = slice(m * E, (m + 1) * E)
                copy_out(w_qkv_r[0][:, :, cols], w_qkv[:, :, cols]).then_inc(wqkv_hi, 1)
            cond_out(1, ps_m[:, :])
            normalise_tokens(0)
            act.wait_ge(l_small, 3 * DMA)
            transpose_out(0)
            act.wait_ge(w_ready, 1)
            q_chunk(0, 0)
            q_chunk(0, 1)
            cond_exp(1)
            k_chunk(0, 0)
            k_chunk(0, 1)
            v_half(0, 0)
            v_half(0, 1)
            normalise_tokens(1)
            softmax_exp(0, 0)
            cond_out(2, ps_a[:, 0:512])
            probs_out(0)

            def tile_step(g, i, norm_ahead, cond_ahead):
                n = GT * g + i
                if i == 0:
                    transpose_out(g + 1)
                if i == 3:
                    if norm_ahead:
                        normalise_tokens(g + 2, (0, 1))
                    attn_out(n)
                    if norm_ahead:
                        normalise_tokens(g + 2, (2, 3))
                if i == 2:
                    v_half(g + 1, 0)
                    v_half(g + 1, 1)
                softmax_exp(n + 1, (i + 1) % 2)
                if cond_ahead and i == 3:
                    cond_out(g + 3, ps_a[:, 0:512])
                if i == 0:
                    q_chunk(g + 1, 0)
                if i == 1:
                    k_chunk(g + 1, 0)
                if i < 3:
                    attn_out(n)
                if norm_ahead and i == 1:
                    cond_exp(g + 2)
                if i == 0:
                    q_chunk(g + 1, 1)
                if i == 1:
                    k_chunk(g + 1, 1)
                probs_out(n + 1)

            with act.Fori(0, NG - 3) as g:
                for i in range(GT):
                    tile_step(g, i, True, True)
            for i in range(GT):
                tile_step(NG - 3, i, True, False)
            act.wait_ge(wqkv_lo, 3)
            act.wait_ge(w_ready, 2)
            for i in range(GT):
                tile_step(NG - 2, i, False, False)
                if i < C:
                    copy_out(w_ih_r[0][:, i, :], w_ih[:, i, :]).then_inc(w_hi, 1)
                elif i == C:
                    copy_out(w_f_r[0][:, :, :], w_f[:, :, :]).then_inc(w_hi, 1)
            n = GT * (NG - 1)
            softmax_exp(n + 1, 1)
            for i in range(GT):
                attn_out(n + i)
                if i + 1 < GT:
                    probs_out(n + i + 1)
                if i + 2 < GT:
                    softmax_exp(n + i + 2, i % 2)

            def gates(t, q, e):
                for gate, dst, mm, done, b0 in (("r", rg, g_r, s_r, 0), ("z", zg, g_z, s_z, 2)):
                    act.wait_ge(mm, t + 1)
                    for c in range(C):
                        nc.scalar.activation(dst[:, c, :], gate_part(gate, q, e, c), ACT.Sigmoid,
                                             bias=brz[:, b0 + c:b0 + c + 1]).then_inc(done, 1)
                for c in range(C):
                    act.wait_ge(npre_done, C * t + c + 1)
                    nc.scalar.activation(ng[:, c, :], npre[:, c, :], ACT.Tanh).then_inc(n_done, 1)

            def round_state(t, q, e):
                act.wait_ge(h_done, C * t + C)
                copy_out(h_r[0][:, q, :, e * B:(e + 1) * B], hT[:, e, :, :]).then_inc(h_hi, 1)

            def round_input(u, q):
                for c in range(C):
                    copy_out(x_r[0][:, q, c, :].rearrange("p (t g b) -> p t g b", t=2, g=NG), step_pair(c, u)
                             ).then_inc(x_hi, 1)

            def pair(u, q, more):
                gates(2 * u, q, 0)
                round_state(2 * u, q, 0)
                if more:
                    round_input(u + 2, q)
                gates(2 * u + 1, q, 1)
                round_state(2 * u + 1, q, 1)

            act.wait_ge(x1_out, C * (B // TB))
            round_input(0, 0)
            round_input(1, 1)
            act.wait_ge(w_ready, 3)
            pair(0, 0, True)
            with act.Fori(0, (PAIRS - 4) // 2) as j:
                pair(2 * j + 1, 1, True)
                pair(2 * j + 2, 0, True)
            pair(PAIRS - 3, 1, True)
            pair(PAIRS - 2, 0, False)
            pair(PAIRS - 1, 1, False)

        @block.vector
        def _(dve):
            def block_sums(k, loaded, n, first=False):
                dve.wait_ge(loaded, n)
                if not first:
                    dve.wait_ge(kw_mm, k)
                for c in range(C):
                    src = xf[:, c, bass.ds(k, 1), :, :].rearrange("p o (n w) b -> p (o n) b w", w=S // NBLK)
                    nc.vector.tensor_reduce(blkT[:, c, :, :].rearrange("p b n -> p n b"), src,
                                            axis=AX_X, op=ALU.add).then_inc(blk_sum, 1)

            block_sums(0, l_xf0[0], DMA, first=True)
            ones = vbd[:, HG, :, :, :].rearrange("p f b (n d) -> p (f b n) d", d=HD)
            dve.wait_ge(l_small, 3 * DMA)
            nc.vector.tensor_tensor(wqr[:, :], row[:, R_Q, :], row[:, R_RMS, :], ALU.mult).then_inc(wq_done, 1)

            def cond_sums(k):
                dve.wait_ge(kw_out, k + 1)
                keys = kw_sb[:, 0, :]
                nc.vector.tensor_tensor_reduce(out=junk[:, 0, :], in0=keys, in1=keys, scale=1.0, scalar=0.0,
                                               op0=ALU.mult, op1=ALU.add, accum_out=ssq[:, :]).then_inc(kw_red, 1)
                nc.vector.tensor_tensor_reduce(out=junk[:, 1, :], in0=keys, in1=wqr[:, :], scale=1.0, scalar=0.0,
                                               op0=ALU.mult, op1=ALU.add, accum_out=dotq[:, :]).then_inc(kw_red, 1)
                dve.wait_ge(kw_red, 2 * k + 2)
                nc.vector.tensor_scalar(rinv[:, :], ssq[:, :], 1.0 / E, EPS, ALU.mult, ALU.add).then_inc(c_mean, 1)

            def cond_scores(k):
                dve.wait_ge(c_pow, k + 1)
                nc.vector.tensor_tensor(cs[:, :], dotq[:, :], rinv[:, :], ALU.mult).then_inc(c_dot, 1)

            row_ps = ps_o[0:1, 320:320 + P].rearrange("g (b n) -> g b n", n=NBLK)
            cTv = cT[:, :].rearrange("g (b n) -> g b n", n=NBLK)

            def cond_shift(k):
                dve.wait_ge(c_row, k + 1)
                nc.vector.tensor_reduce(cmx[:, :], row_ps, axis=AX_X, op=ALU.max).then_inc(c_max, 1)
                dve.wait_ge(c_max, k + 1)
                nc.vector.tensor_tensor(cTv, row_ps, cmx[:, :].unsqueeze(2).to_broadcast([1, GB, NBLK]),
                                        ALU.subtract).then_inc(c_sub, 1)

            def cond_normalise(k):
                dve.wait_ge(c_exp, k + 1)
                nc.vector.tensor_reduce(csum[:, :], cTv, axis=AX_X, op=ALU.add).then_inc(c_sum, 1)
                dve.wait_ge(c_sum, k + 1)
                nc.vector.reciprocal(csum[:, :], csum[:, :]).then_inc(c_inv, 1)
                dve.wait_ge(c_inv, k + 1)
                nc.vector.tensor_tensor(cTv, cTv, csum[:, :].unsqueeze(2).to_broadcast([1, GB, NBLK]),
                                        ALU.mult).then_inc(c_wt, 1)

            def select_blocks(k):
                dve.wait_ge(c_col, k + 1)
                nc.vector.tensor_scalar(ra[:, :], spread, ps_o[:, 320 + P:321 + P], None,
                                        ALU.mult).then_inc(ra_ready, 1)

            def add_proj(k):
                dve.wait_ge(l_xg, DMA * (k + 1))
                for h in range(2):
                    dve.wait_ge(r_mm, 2 * k + h + 1)
                    if h == 0:
                        dve.wait_ge(yt_mm, C * k)
                    nc.vector.tensor_tensor(y[:, 2 * h:2 * h + 2, :].rearrange("p t e -> p (t e)"),
                                            xg[:, 2 * h:2 * h + 2, :].rearrange("p t e -> p (t e)"),
                                            ps_a[:, h * 512:(h + 1) * 512], ALU.add).then_inc(z_done, 1)
                for i in range(GT):
                    dve.wait_ge(z_done, 2 * k + i // 2 + 1)
                    last = nc.vector.bn_stats(st[:, i, :], y[:, i, :])
                last.then_inc(bn_done, 1)

            def mean_and_variance(k):
                dve.wait_ge(bn_done, 2 * k + 1)
                nc.vector.memset(carrier[:, 2:3], 0.0)
                for i in range(GT):
                    last = nc.vector.bn_aggr(mv[:, i, :], st[:, i, :])
                last.then_inc(bn_done, 1)

            def rest_of_weights(m):
                cols = slice(m * E, (m + 1) * E)
                dve.wait_ge(wqkv_hi, m + 1)
                nc.vector.tensor_tensor(w_qkv_r[1][:, :, cols], w_qkv[:, :, cols], w_qkv_r[0][:, :, cols],
                                        ALU.subtract).then_inc(wqkv_lo, 1)

            def halves(p):
                def view(a, h):
                    return a[:, h * 512:(h + 1) * 512].rearrange("p (h k) -> p h k", k=S)
                return [(h, view(masked, h), view(sc[:, p, :], h), mx[:, p, h * NH // 2:(h + 1) * NH // 2])
                        for h in range(2)]

            def softmax_mask(n, p, first=False):
                for h, kept, _, _ in halves(p):
                    if not first:
                        dve.wait_ge(sc_sub, 2 * n - 1 + h)
                    dve.wait_ge(sc_mm, 2 * n + h + 1)
                    nc.vector.memset(carrier[:, h:h + 1], 0.0)
                    nc.vector.copy_predicated(kept, keep.unsqueeze(1).to_broadcast([P, NH // 2, S]),
                                              ps_s[:, h * 512:(h + 1) * 512].rearrange("p (h k) -> p h k", k=S)
                                              ).then_inc(sc_out, 1)

            def softmax_shift(n, p):
                for h, kept, _, m in halves(p):
                    dve.wait_ge(sc_out, 2 * n + h + 1)
                    nc.vector.tensor_reduce(m, kept, axis=AX_X, op=ALU.max).then_inc(sc_max, 1)
                for h, kept, shifted, m in halves(p):
                    dve.wait_ge(sc_max, 2 * n + h + 1)
                    nc.vector.tensor_tensor(shifted, kept, m.unsqueeze(2).to_broadcast([P, NH // 2, S]),
                                            ALU.subtract).then_inc(sc_sub, 1)

            def normalise(n):
                dve.wait_ge(pv_mm, n + 1)
                o5 = ps_o[:, 0:NQ * 40].rearrange("p (q s d) -> p q s d", q=NQ, s=HG + 1)
                nc.vector.reciprocal(rden[:, :].rearrange("p (q s) -> p q s", s=HG),
                                     o5[:, :, HG, 0:HG]).then_inc(den_inv, 1)
                dve.wait_ge(den_inv, n + 1)
                nc.vector.tensor_tensor(
                    on[:, :].rearrange("p (q s d) -> p q s d", q=NQ, s=HG), o5[:, :, 0:HG, :],
                    rden[:, :].rearrange("p (q s) -> p q s", s=HG).unsqueeze(3).to_broadcast([P, NQ, HG, HD]),
                    ALU.mult).then_inc(o_norm, 1)

            def residual(n, g, i):
                dve.wait_ge(x1_mm, n + 1)
                for c in range(C):
                    xs = xf[:, c, bass.ds(g, 1), :, i * TB:(i + 1) * TB].rearrange("p o t b -> p (o b) t")
                    nc.vector.scalar_tensor_tensor(
                        xs, ps_m[:, E + c * P:E + (c + 1) * P].rearrange("p (b t) -> p b t", b=TB),
                        b_out[:, c:c + 1], xs, ALU.add, ALU.add).then_inc(x1_out, 1)

            dve.wait_ge(wq_done, 1)
            cond_sums(0)
            nc.vector.tensor_copy(masked[:, :].rearrange("p (h k) -> p h k", k=S), kst[:, K_FILL:K_FILL + S].unsqueeze(
                1).to_broadcast([P, NH, S])).then_inc(filled, 1)
            cond_scores(0)
            cond_shift(0)
            cond_normalise(0)
            select_blocks(0)
            nc.vector.memset(ones, 0.0).then_inc(filled, 1)
            rest_of_weights(0)
            block_sums(1, l_xf0[1], DMA)
            add_proj(0)
            mean_and_variance(0)
            nc.vector.tensor_scalar(bq[:, :], vec[:, V_BQ:V_BQ + C], SCALE, None, ALU.mult).then_inc(w_ready, 1)
            rest_of_weights(1)
            rest_of_weights(2)
            dve.wait_ge(filled, 2)
            for h in range(HG):
                slot = ones[32 * h:32 * h + 32, :, h:h + 1]
                last = nc.vector.tensor_copy(slot, key_factor[32 * h:32 * h + 32, :].unsqueeze(1).to_broadcast(
                    [32, GT * TB * NQ, 1]))
            last.then_inc(zeroed, 1)
            cond_sums(1)
            cond_scores(1)
            cond_shift(1)
            cond_normalise(1)
            dve.wait_ge(bv_mm, 1)
            nc.vector.tensor_tensor(b_out[:, :], ps_s[:, 0:C], vec[:, V_BPROJ:V_BPROJ + C],
                                    ALU.add).then_inc(b_out_done, 1)
            select_blocks(1)
            block_sums(2, l_xf0[2], DMA)
            add_proj(1)
            mean_and_variance(1)
            softmax_mask(0, 0, first=True)
            softmax_shift(0, 0)

            dve.wait_ge(l_gru, 4 * DMA)
            nc.vector.tensor_tensor(w_f[:, :, :], w_f[:, :, :],
                                    row[:, R_FSC, :].unsqueeze(1).to_broadcast([P, C, E]),
                                    ALU.mult).then_inc(w_ready, 1)
            nc.vector.tensor_tensor(brz[:, :], vec[:, V_BIH:V_BIH + 4], vec[:, V_BHH:V_BHH + 4],
                                    ALU.add).then_inc(w_ready, 1)

            def rest_of_gru_weights(i):
                w, w_r = (w_ih[:, i, :], [r[:, i, :] for r in w_ih_r]) if i < C else (
                    w_f[:, :, :], [r[:, :, :] for r in w_f_r])
                dve.wait_ge(w_hi, i + 1)
                nc.vector.tensor_tensor(w_r[1], w, w_r[0], ALU.subtract).then_inc(w_lo, 1)

            def tile_step(g, i, norm_ahead, cond_ahead):
                n = GT * g + i
                softmax_mask(n + 1, (i + 1) % 2)
                if norm_ahead and i == 2:
                    select_blocks(g + 2)
                if i == 3:
                    normalise(n)
                softmax_shift(n + 1, (i + 1) % 2)
                if i < 3:
                    normalise(n)
                if norm_ahead and i == 0:
                    cond_sums(g + 2)
                if norm_ahead and i == 1:
                    cond_shift(g + 2)
                if cond_ahead and i == 1:
                    block_sums(g + 3, l_xf, DMA * (g + 1))
                if norm_ahead and i == 1:
                    cond_normalise(g + 2)
                if norm_ahead and i == 2:
                    add_proj(g + 2)
                    mean_and_variance(g + 2)
                if not norm_ahead and 0 < i:
                    rest_of_gru_weights(i - 1)
                residual(n, g, i)
                if norm_ahead and i == 0:
                    cond_scores(g + 2)

            with dve.Fori(0, NG - 3) as g:
                for i in range(GT):
                    tile_step(g, i, True, True)
            for i in range(GT):
                tile_step(NG - 3, i, True, False)
            for i in range(GT):
                tile_step(NG - 2, i, False, False)
            n = GT * (NG - 1)
            softmax_mask(n + 1, 1)
            normalise(n)
            softmax_shift(n + 1, 1)
            for i in range(GT):
                if i > 0:
                    normalise(n + i)
                if i + 2 < GT:
                    softmax_mask(n + i + 2, i % 2)
                    softmax_shift(n + i + 2, i % 2)
                residual(n + i, NG - 1, i)

            def state(t, q, e):
                old, new = hT[:, 1 - e, :, :], hT[:, e, :, :]
                dve.wait_ge(g_n, t + 1)
                for c in range(C):
                    dve.wait_ge(s_r, C * t + c + 1)
                    nc.vector.scalar_tensor_tensor(rg[:, c, :], ps_o[:, c * B:(c + 1) * B],
                                                   vec[:, V_BHH + 4 + c:V_BHH + 5 + c], rg[:, c, :],
                                                   ALU.add, ALU.mult).then_inc(rh_done, 1)
                for c in range(C):
                    dve.wait_ge(rh_done, C * t + c + 1)
                    nc.vector.scalar_tensor_tensor(npre[:, c, :], gate_part("n", q, e, c),
                                                   vec[:, V_BIH + 4 + c:V_BIH + 5 + c], rg[:, c, :],
                                                   ALU.add, ALU.add).then_inc(npre_done, 1)
                dve.wait_ge(s_z, C * t + C)
                nc.vector.tensor_scalar(zc[:, :, :], zg[:, :, :], -1.0, 1.0, ALU.mult, ALU.add).then_inc(zc_done, 1)
                nc.vector.tensor_tensor(zh[:, :, :], zg[:, :, :], old, ALU.mult).then_inc(zh_done, 1)
                dve.wait_ge(zc_done, t + 1)
                for c in range(C):
                    dve.wait_ge(n_done, C * t + c + 1)
                    nc.vector.tensor_tensor(ng[:, c, :], ng[:, c, :], zc[:, c, :], ALU.mult).then_inc(nz_done, 1)
                dve.wait_ge(zh_done, t + 1)
                for c in range(C):
                    dve.wait_ge(nz_done, C * t + c + 1)
                    nc.vector.tensor_tensor(new[:, c, :], ng[:, c, :], zh[:, c, :], ALU.add).then_inc(h_done, 1)

            def rest_of_state(t, q, e):
                part = slice(e * B, (e + 1) * B)
                dve.wait_ge(h_hi, t + 1)
                nc.vector.tensor_tensor(h_r[1][:, q, :, part], hT[:, e, :, :], h_r[0][:, q, :, part],
                                        ALU.subtract).then_inc(h_lo, 1)

            def rest_of_input(u, q):
                for c in range(C):
                    dve.wait_ge(x_hi, C * u + c + 1)
                    lo, hi = (x[:, q, c, :].rearrange("p (t g b) -> p t g b", t=2, g=NG) for x in (x_r[1], x_r[0]))
                    nc.vector.tensor_tensor(lo, step_pair(c, u), hi, ALU.subtract).then_inc(x_lo, 1)

            def emit(u, q):
                dve.wait_ge(f_mm, u + 1)
                for c in range(C):
                    for e in range(2):
                        cols = slice((2 * c + e) * B, (2 * c + e + 1) * B)
                        nc.vector.scalar_tensor_tensor(
                            ost[:, q, c, e * B:(e + 1) * B].rearrange("p (g b) -> p g b", g=NG),
                            ps_m[:, cols].rearrange("p (g b) -> p g b", g=NG), vec[:, V_FFNB + c:V_FFNB + c + 1],
                            xf[:, c, :, bass.ds(2 * u + e, 1), :].rearrange("p g o b -> p g (o b)"),
                            ALU.add, ALU.add).then_inc(f_out, 1)

            def pair(u, q, more, stores=None, first=False):
                state(2 * u, q, 0)
                rest_of_state(2 * u, q, 0)
                if stores is not None:
                    dve.wait_ge(stored[1 - q], DMA * stores)
                if not first:
                    emit(u - 1, 1 - q)
                state(2 * u + 1, q, 1)
                rest_of_state(2 * u + 1, q, 1)
                if more:
                    rest_of_input(u + 2, q)

            dve.wait_ge(x1_out, C * (B // TB))
            rest_of_input(0, 0)
            rest_of_input(1, 1)
            pair(0, 0, True, first=True)
            pair(1, 1, True)
            pair(2, 0, True)
            with dve.Fori(1, (PAIRS - 4) // 2) as j:
                pair(2 * j + 1, 1, True, stores=j)
                pair(2 * j + 2, 0, True, stores=j)
            pair(PAIRS - 3, 1, True, stores=PAIRS // 2 - 2)
            pair(PAIRS - 2, 0, False, stores=PAIRS // 2 - 2)
            pair(PAIRS - 1, 1, False, stores=PAIRS // 2 - 1)
            dve.wait_ge(stored[1], DMA * (PAIRS // 2 - 1))
            emit(PAIRS - 1, 1)

        @block.tensor
        def _(pe):
            def block_product(k, bank, c):
                pe.wait_ge(blk_sum, C * k + C)
                last = nc.tensor.matmul(bank, blkT[:, c, :, :].rearrange("p b n -> p (b n)"), w_kwo[:, c, :],
                                        start=(c == 0), stop=(c == C - 1))
                if c == C - 1:
                    last.then_inc(kw_mm, 1)

            def block_products(k, bank):
                for c in range(C):
                    block_product(k, bank, c)

            def cond_row(k):
                pe.wait_ge(c_dot, k + 1)
                nc.tensor.matmul(ps_o[0:1, 320:320 + P], cs[:, :], ident, start=True, stop=True).then_inc(c_row, 1)

            def cond_col(k):
                pe.wait_ge(c_wt, k + 1)
                nc.tensor.matmul(ps_o[:, 320 + P:321 + P], cT[:, :], ident[0:1, 0:1],
                                 start=True, stop=True).then_inc(c_col, 1)

            def spread_proj(k):
                pe.wait_ge(ra_ready, k + 1)
                for i in range(GT):
                    last = nc.tensor.matmul(ps_a[:, i * E:(i + 1) * E], ra[:, i * P:(i + 1) * P],
                                            kw_sb[:, 1, :],
                                            start=True, stop=True)
                    if i % 2:
                        last.then_inc(r_mm, 1)

            def transpose_y(k, sums_ahead=True):
                pe.wait_ge(z_done, 2 * k + 2)
                if sums_ahead:
                    pe.wait_ge(kw_out, k + 2)
                for c in range(C):
                    for i in range(GT):
                        pe.wait_ge(y_done, GT * k + i + 1)
                        last = nc.tensor.transpose(ps_a[:, c * 512 + i * P:c * 512 + (i + 1) * P],
                                                   y[:, i, c * P:(c + 1) * P], ident)
                    last.then_inc(yt_mm, 1)

            def project_qk(k, first_col, done, m):
                bank = ps_a[:, m * GC:(m + 1) * GC]
                for a, b in ((0, 0), (1, 0), (0, 1)):
                    if b == 1:
                        pe.wait_ge(yt_lo, C * k + C)
                    for c in range(C):
                        last = nc.tensor.matmul(bank, w_qkv_r[a][:, c, first_col + m * P:first_col + (m + 1) * P],
                                                yT_r[b][:, c, :], start=(a == b == c == 0),
                                                stop=(b == 1 and c == C - 1))
                last.then_inc(done, 1)

            def project_v(k, h):
                for i in (2 * h, 2 * h + 1):
                    for c in range(C):
                        for a, b in ((0, 0), (1, 0), (0, 1)):
                            last = nc.tensor.matmul(ps_a[:, i * E:(i + 1) * E], yT_r[a][:, c, i * P:(i + 1) * P],
                                                    w_qkv_r[b][:, c, 2 * E:3 * E], start=(a == b == c == 0),
                                                    stop=(b == 1 and c == C - 1))
                last.then_inc(v_mm, 1)

            def value_bias():
                for m in range(C):
                    for c in range(C):
                        last = nc.tensor.matmul(ps_s[:, m:m + 1], w_p[:, c, m * P:(m + 1) * P],
                                                vec[:, V_BV + c:V_BV + c + 1], start=(c == 0), stop=(c == C - 1))
                last.then_inc(bv_mm, 1)

            def work_ahead(k, i, h):
                if i == 0:
                    pe.wait_ge(yt_hi, C * k + C)
                    pe.wait_ge(yt_out, C * k + h + 1)
                    project_qk(k, 0, q_mm, h)
                elif i == 1:
                    pe.wait_ge(q_out, 2 * k + h + 1)
                    project_qk(k, E, k_mm, h)
                elif i == 2:
                    pe.wait_ge(k_out, 2 * k + h + 1)
                    project_v(k, h)

            def scores(n, g, i, first=False):
                pe.wait_ge(k_in[i // 2], HG * DMA * (g + 1))
                pe.wait_ge(q_in[i // 2], TB * DMA * (g + 1))
                for h in range(2):
                    if not first:
                        pe.wait_ge(sc_out, 2 * n - 1 + h)
                    bank = ps_s[:, h * 512:(h + 1) * 512]
                    for q in range(HW):
                        cols = slice(i % TH * S, (i % TH + 1) * S)
                        tile_q = qbd[:, i // TH, h * HW + q, :, :].rearrange("p b (s t) -> p t (b s)", t=TH)
                        last = nc.tensor.matmul(bank[:, q * P:(q + 1) * P], tile_q[:, i % TH, :],
                                                kbd[:, :, i // TH, h * HW + q, cols],
                                                start=True, stop=True)
                    last.then_inc(sc_mm, 1)

            def transpose_probs(n, p, first=False):
                for h in range(2):
                    pe.wait_ge(sc_exp, 2 * n + h + 1)
                    if not first:
                        pe.wait_ge(pt_out, 2 * n - 1 + h)
                    for q in range(HW):
                        col = (h * HW + q) * P
                        last = nc.tensor.transpose(ps_t[:, col:col + P], sc[:, p, col:col + P], ident)
                    last.then_inc(pt_mm, 1)

            def probs_v(n, g, i):
                pe.wait_ge(v_in[i // 2], HG * DMA * (g + 1))
                pe.wait_ge(pt_out, 2 * n + 2)
                for q in range(NQ):
                    for b in range(TB):
                        col = i % TH * VW + q * HD
                        last = nc.tensor.matmul(
                            ps_o[32 * b:32 * b + 32, q * 40:(q + 1) * 40], pT[:, q, 32 * b:32 * b + 32],
                            vbd[:, :, i // TH, b, col:col + HD],
                            start=True, stop=True, tile_position=(0, 32 * b))
                last.then_inc(pv_mm, 1)

            def transpose_attn(n):
                pe.wait_ge(o_norm, n + 1)
                for c in range(C):
                    last = nc.tensor.transpose(ps_m[:, c * P:(c + 1) * P], on[:, c * P:(c + 1) * P], ident)
                last.then_inc(ot_mm, 1)

            def project_out(n):
                pe.wait_ge(ot_out, n + 1)
                for m in range(C):
                    for c in range(C):
                        last = nc.tensor.matmul(ps_m[:, E + m * P:E + (m + 1) * P], w_p[:, c, m * P:(m + 1) * P],
                                                oT[:, c, :], start=(c == 0), stop=(c == C - 1))
                last.then_inc(x1_mm, 1)

            def keep_warm(products):
                for _ in range(products):
                    nc.tensor.matmul(ps_t[:, 0:256], oT[:, 0, :], oT[:, :, :].rearrange("p c n -> p (c n)"),
                                     start=True, stop=True)

            pe.wait_ge(warm_zeros, 1)
            keep_warm(6)
            pe.wait_ge(l_kwo, DMA)
            block_products(0, ps_a[:, 0:512])
            keep_warm(5)
            pe.wait_ge(l_small, 3 * DMA)
            cond_row(0)
            keep_warm(4)
            cond_col(0)
            spread_proj(0)
            block_products(1, ps_m[:, :])
            transpose_y(0, False)
            pe.wait_ge(wqkv_lo, 3)
            work_ahead(0, 0, 0)
            work_ahead(0, 0, 1)
            cond_row(1)
            work_ahead(0, 1, 0)
            work_ahead(0, 1, 1)
            cond_col(1)
            value_bias()
            work_ahead(0, 2, 0)
            work_ahead(0, 2, 1)
            pe.wait_ge(v_out, 2)
            spread_proj(1)
            pe.wait_ge(b_out_done, 1)
            keep_warm(12)
            scores(0, 0, 0, first=True)
            pe.wait_ge(z_done, 4)
            block_products(2, ps_a[:, 0:512])
            transpose_probs(0, 0, first=True)

            def tile_step(g, i, norm_ahead, cond_ahead):
                n = GT * g + i
                if i == 0:
                    transpose_y(g + 1, norm_ahead)
                scores(n + 1, g + (i + 1) // GT, (i + 1) % GT)
                if norm_ahead and i == 1:
                    cond_row(g + 2)
                if norm_ahead and i == 2:
                    cond_col(g + 2)
                if i == 2:
                    work_ahead(g + 1, i, 0)
                    work_ahead(g + 1, i, 1)
                if norm_ahead and i == 2:
                    pe.wait_ge(ra_ready, g + 3)
                probs_v(n, g, i)
                if norm_ahead and i == 2:
                    pe.wait_ge(v_out, 2 * g + 4)
                    spread_proj(g + 2)
                if i < 2:
                    work_ahead(g + 1, i, 0)
                    work_ahead(g + 1, i, 1)
                if cond_ahead and i == 3:
                    pe.wait_ge(z_done, 2 * g + 6)
                    block_product(g + 3, ps_a[:, 0:512], 0)
                transpose_attn(n)
                if cond_ahead and i == 3:
                    block_product(g + 3, ps_a[:, 0:512], 1)
                if i == 3:
                    project_out(n)
                transpose_probs(n + 1, (i + 1) % 2)
                if i < 3:
                    project_out(n)

            with pe.Fori(0, NG - 3) as g:
                for i in range(GT):
                    tile_step(g, i, True, True)
            for g in (NG - 3, NG - 2):
                for i in range(GT):
                    tile_step(g, i, g < NG - 2, False)
            g, n = NG - 1, GT * (NG - 1)
            scores(n + 1, g, 1)
            for i in range(GT):
                probs_v(n + i, g, i)
                if i + 2 < GT:
                    scores(n + i + 2, g, i + 2)
                transpose_attn(n + i)
                if i + 1 < GT:
                    transpose_probs(n + i + 1, (i + 1) % 2)
                project_out(n + i)

            def exact_product(bank, w_r, col, rhs_r):
                first = True
                for m in range(C):
                    for c in range(C):
                        for a, b in ((0, 0), (0, 1), (1, 0)):
                            last = nc.tensor.matmul(bank[:, m * 2 * B:(m + 1) * 2 * B],
                                                    w_r[a][:, c, col + m * P:col + (m + 1) * P], rhs_r[b][:, c, :],
                                                    start=first, stop=(c == C - 1 and a == 1), skip_group_check=True)
                            first = False
                return last

            def from_input(u, q, gates):
                for gate, col in gates:
                    exact_product(gate_bank(gate, q), w_ih_r, col, [x[:, q, :, :] for x in x_r])

            R_GATE, Z_GATE, N_GATE = ("r", 0), ("z", E), ("n", 2 * E)

            def from_state(q, e, gates=("r", None, "z")):
                old = hT[:, 1 - e, :, :]
                for which in gates:
                    done = {"r": g_r, None: g_n, "z": g_z}[which]
                    col = {"r": 0, "z": E, None: 2 * E}[which]
                    for c in range(C):
                        for m in range(C):
                            dst = gate_part(which, q, e, m) if which else ps_o[:, m * B:(m + 1) * B]
                            last = nc.tensor.matmul(dst, w_hh[:, c, col + m * P:col + (m + 1) * P], old[:, c, :],
                                                    start=(which is None and c == 0 and m == 0), stop=(c == C - 1),
                                                    skip_group_check=True)
                    last.then_inc(done, 1)

            def ffn(u, q):
                pe.wait_ge(h_lo, 2 * u + 2)
                exact_product(ps_m[:, :], w_f_r, 0, [h[:, q, :, :] for h in h_r]).then_inc(f_mm, 1)

            def pair(u, q, ahead, first=False):
                if first:
                    from_state(q, 0, ("r", "z"))
                else:
                    pe.wait_ge(h_done, 2 * C * u)
                    from_state(q, 0)
                    ffn(u - 1, 1 - q)
                if ahead:
                    pe.wait_ge(x_lo, C * u + 2 * C)
                    from_input(u + 1, 1 - q, (R_GATE,))
                pe.wait_ge(h_done, 2 * C * u + C)
                from_state(q, 1)
                if ahead:
                    from_input(u + 1, 1 - q, (Z_GATE, N_GATE))

            pe.wait_ge(l_gru, 4 * DMA)
            from_state(0, 0, (None,))
            pe.wait_ge(x1_out, C * (B // TB))
            pe.wait_ge(w_lo, C + 1)
            pe.wait_ge(x_lo, C)
            from_input(0, 0, (R_GATE, Z_GATE, N_GATE))
            pair(0, 0, True, first=True)
            with pe.Fori(0, (PAIRS - 2) // 2) as j:
                pair(2 * j + 1, 1, True)
                pair(2 * j + 2, 0, True)
            pair(PAIRS - 1, 1, False)
            ffn(PAIRS - 1, 1)


def kernel(x, cond_2048, L0_cond_rms_weight, L0_cond_Wk, L0_cond_Wo, L0_cond_ln_gamma, L0_cond_ln_beta,
           L0_attn_W_attn, L0_attn_b_attn, L0_attn_W_proj, L0_attn_b_proj, L0_cond2_W_ih, L0_cond2_W_hh,
           L0_cond2_b_ih, L0_cond2_b_hh, L0_ffn_weight, L0_ffn_scale_weight, L0_ffn_bias):
    import concourse.bacc as bacc
    from concourse.bass_utils import run_bass_kernel_spmd

    a = {k: np.asarray(v) for k, v in locals().items() if not k.startswith("b") or k.startswith("b_")}
    x, cond = a["x"], a["cond_2048"]
    wa, ba = a["L0_attn_W_attn"], a["L0_attn_b_attn"]

    def chunks(w):
        return w.reshape(C, P, -1).transpose(1, 0, 2)

    def qk_cols(w):
        return w.reshape(-1, NQ, HG, HD).transpose(0, 3, 2, 1).reshape(-1, E)

    def v_cols(w):
        return w.reshape(-1, NQ, HG, HD).transpose(0, 2, 1, 3).reshape(-1, E)

    def feature(v):
        return v.reshape(-1, P).T

    vecs = np.concatenate([feature(a[n]) for n in (
        "L0_cond_ln_gamma", "L0_cond_ln_beta", "L0_attn_b_proj", "L0_ffn_bias", "L0_cond2_b_ih", "L0_cond2_b_hh")]
        + [feature(qk_cols(ba[0:E])[0]), feature(qk_cols(ba[E:2 * E])[0]), feature(ba[2 * E:])], 1)
    rows = np.stack([cond[1], a["L0_cond_rms_weight"], a["L0_ffn_scale_weight"]])
    ins = {
        "x_tok": x.reshape(B * S // P, P, E),
        "x_feat": x.reshape(NG, GB, S, C, P).transpose(0, 4, 3, 2, 1).reshape(NG, P, C, S * GB),
        "cond_t": chunks(cond.T),
        "wkwo": np.concatenate([chunks(a["L0_cond_Wk"].T), chunks(a["L0_cond_Wo"].T)], 2),
        "wqkv": np.concatenate([chunks(qk_cols(wa[:, 0:E])), chunks(qk_cols(wa[:, E:2 * E])),
                                chunks(v_cols(wa[:, 2 * E:]))], 2),
        "wp": chunks(a["L0_attn_W_proj"]),
        "wih": chunks(a["L0_cond2_W_ih"]),
        "whh": chunks(a["L0_cond2_W_hh"]),
        "wf": chunks(a["L0_ffn_weight"].T),
        "vecs": vecs,
        "rows": np.broadcast_to(rows[None], (P, NROW, E)),
        "consts": shape_constants(),
    }
    nc = bacc.Bacc("TRN2", target_bir_lowering=False, num_devices=1)
    arrays, args = {}, []
    for name, v in ins.items():
        v = np.ascontiguousarray(v)
        arrays["in_" + name] = v
        args.append(nc.dram_tensor("in_" + name, v.shape, mybir.dt.from_np(v.dtype), kind="ExternalInput").ap())
    out = nc.dram_tensor("out_feat", (PAIRS, P, C, 2 * B), F32, kind="ExternalOutput").ap()
    q_dram, k_dram = (nc.dram_tensor(n, (NG, GH * TB, E, HT), F32, kind="Internal").ap() for n in ("q_dram", "k_dram"))
    v_dram = nc.dram_tensor("v_dram", (NG, GH, HG, P, TH * VW), F32, kind="Internal").ap()
    adaln_attn_gru_ffn(nc, *args, q_dram, k_dram, v_dram, out)
    r = run_bass_kernel_spmd(nc, [arrays], core_ids=[0])
    got = r.results[0]["out_feat"]
    return got.reshape(PAIRS, P, C, 2, B).transpose(4, 0, 3, 2, 1).reshape(B, S, E)
```
